# Optimizing a Trainium2 kernel written in Bass

```python
import numpy as np
import jax
import jax.numpy as jnp

def _softmax(x, axis=-1):
    return jax.nn.softmax(x, axis=axis)

def _gelu(x):
    return jax.nn.gelu(x, approximate=True)

def _silu(x):
    return jax.nn.silu(x)

def _sigmoid(x):
    return jax.nn.sigmoid(x)

def _layernorm(x, axis=-1, eps=1e-05):
    m = jnp.mean(x, axis=axis, keepdims=True)
    v = jnp.var(x, axis=axis, keepdims=True)
    return (x - m) / jnp.sqrt(v + eps)

def _scatter_add(tgt, idx, src, axis=0):
    return tgt.at[idx].add(src)

def _segment_sum(src, seg, n):
    return jax.ops.segment_sum(src, seg, n)
kernel_name = 'mk_macaron_d1_jaxref_r8_bac1ad'

def setup_inputs(seed: int=0):
    np.random.seed(seed)
    _w = jnp.asarray

    def _L0_attn_setup():
        import jax, jax.numpy as jnp
        import numpy as np
        N_HEADS = 16
        EPS = 1e-06
        key = jax.random.key(seed)
        ks = jax.random.split(key, 10)
        B, T, D = (2, 256, 128)
        x = jax.random.normal(ks[0], (B, T, D), dtype=jnp.float32)
        norm_w = jnp.ones((D,), dtype=jnp.float32)
        bound = float(np.sqrt(6.0 / (D + D)))

        def lin(k):
            return jax.random.uniform(k, (D, D), dtype=jnp.float32, minval=-bound, maxval=bound)
        Wq, Wk, Wv, Wo = (lin(ks[1]), lin(ks[2]), lin(ks[3]), lin(ks[4]))
        bq = jnp.zeros((D,), dtype=jnp.float32)
        bk = jnp.zeros((D,), dtype=jnp.float32)
        bv = jnp.zeros((D,), dtype=jnp.float32)
        bo = jnp.zeros((D,), dtype=jnp.float32)
        return {'x': x, 'norm_w': norm_w, 'Wq': Wq, 'bq': bq, 'Wk': Wk, 'bk': bk, 'Wv': Wv, 'bv': bv, 'Wo': Wo, 'bo': bo}
    _L0_attn_in = _L0_attn_setup()

    def _L0_ffn_setup():
        import jax, jax.numpy as jnp
        import numpy as np
        D_MODEL = 128
        MLP_DIM = 512
        N_EXPERTS = 8
        B, T = (4, 128)
        key = jax.random.key(seed)
        ks = jax.random.split(key, 7)
        scale_in = (1.0 / D_MODEL) ** 0.5
        scale_out = (1.0 / MLP_DIM) ** 0.5
        bound_g = (1.0 / D_MODEL) ** 0.5
        w_gate = jax.random.uniform(ks[0], (D_MODEL, N_EXPERTS), minval=-bound_g, maxval=bound_g, dtype=jnp.float32)
        b_gate = jax.random.uniform(ks[1], (N_EXPERTS,), minval=-bound_g, maxval=bound_g, dtype=jnp.float32)
        W1 = jax.random.uniform(ks[2], (N_EXPERTS, D_MODEL, MLP_DIM), minval=-scale_in, maxval=scale_in, dtype=jnp.float32)
        b1 = jnp.zeros((N_EXPERTS, MLP_DIM), dtype=jnp.float32)
        W2 = jax.random.uniform(ks[3], (N_EXPERTS, MLP_DIM, D_MODEL), minval=-scale_out, maxval=scale_out, dtype=jnp.float32)
        b2 = jnp.zeros((N_EXPERTS, D_MODEL), dtype=jnp.float32)
        x = jax.random.normal(ks[4], (B, T, D_MODEL), dtype=jnp.float32)
        return {'x': x, 'w_gate': w_gate, 'b_gate': b_gate, 'W1': W1, 'b1': b1, 'W2': W2, 'b2': b2}
    _L0_ffn_in = _L0_ffn_setup()
    _d = {'L0_attn_x': _L0_attn_in['x'], 'L0_attn_norm_w': _L0_attn_in['norm_w'], 'L0_attn_Wq': _L0_attn_in['Wq'], 'L0_attn_bq': _L0_attn_in['bq'], 'L0_attn_Wk': _L0_attn_in['Wk'], 'L0_attn_bk': _L0_attn_in['bk'], 'L0_attn_Wv': _L0_attn_in['Wv'], 'L0_attn_bv': _L0_attn_in['bv'], 'L0_attn_Wo': _L0_attn_in['Wo'], 'L0_attn_bo': _L0_attn_in['bo'], 'L0_ffn_w_gate': _L0_ffn_in['w_gate'], 'L0_ffn_b_gate': _L0_ffn_in['b_gate'], 'L0_ffn_W1': _L0_ffn_in['W1'], 'L0_ffn_b1': _L0_ffn_in['b1'], 'L0_ffn_W2': _L0_ffn_in['W2'], 'L0_ffn_b2': _L0_ffn_in['b2']}
    _x0 = _d['L0_attn_x']
    _d['L0_attn_x'] = jax.random.normal(jax.random.fold_in(jax.random.key(seed), 1), (8, 256, 128), dtype=_x0.dtype)
    del _x0
    return _d

def reference(L0_attn_x, L0_attn_norm_w, L0_attn_Wq, L0_attn_bq, L0_attn_Wk, L0_attn_bk, L0_attn_Wv, L0_attn_bv, L0_attn_Wo, L0_attn_bo, L0_ffn_w_gate, L0_ffn_b_gate, L0_ffn_W1, L0_ffn_b1, L0_ffn_W2, L0_ffn_b2):

    def _L0_attn_ref(x, norm_w, Wq, bq, Wk, bk, Wv, bv, Wo, bo):
        import jax, jax.numpy as jnp
        import numpy as np
        N_HEADS = 16
        EPS = 1e-06
        B, T, D = x.shape
        H = N_HEADS
        hd = D // H
        xn = x * jax.lax.rsqrt(jnp.mean(x * x, axis=-1, keepdims=True) + EPS) * norm_w
        q = (xn @ Wq.T + bq).reshape(B, T, H, hd).transpose(0, 2, 1, 3)
        k = (xn @ Wk.T + bk).reshape(B, T, H, hd).transpose(0, 2, 1, 3)
        v = (xn @ Wv.T + bv).reshape(B, T, H, hd).transpose(0, 2, 1, 3)
        scale = 1.0 / jnp.sqrt(jnp.asarray(hd, dtype=x.dtype))
        scores = jnp.einsum('bhqd,bhkd->bhqk', q, k) * scale
        causal = jnp.triu(jnp.ones((T, T), dtype=bool), k=1)
        scores = jnp.where(causal, jnp.asarray(-jnp.inf, dtype=scores.dtype), scores)
        attn = jax.nn.softmax(scores, axis=-1)
        out = jnp.einsum('bhqk,bhkd->bhqd', attn, v)
        out = out.transpose(0, 2, 1, 3).reshape(B, T, D)
        out = out @ Wo.T + bo
        return xn + out

    def _L0_ffn_ref(x, w_gate, b_gate, W1, b1, W2, b2):
        import jax, jax.numpy as jnp
        import numpy as np
        D_MODEL = 128
        MLP_DIM = 512
        N_EXPERTS = 8
        B, T = (4, 128)
        b, t, d = x.shape
        x_flat = x.reshape(b * t, d)
        logits = x_flat @ w_gate + b_gate
        probs = jax.nn.softmax(logits, axis=-1)
        route_p = jnp.max(probs, axis=-1)
        route_idx = jnp.argmax(probs, axis=-1)
        h = jnp.einsum('nd,edm->enm', x_flat, W1) + b1[:, None, :]
        h = jax.nn.relu(h)
        y = jnp.einsum('enm,emd->end', h, W2) + b2[:, None, :]
        n = b * t
        out = y[route_idx, jnp.arange(n)] * route_p[:, None]
        return out.reshape(b, t, d)
    x = L0_attn_x
    x = x + 0.5 * _L0_ffn_ref(_layernorm(x, axis=-1), L0_ffn_w_gate, L0_ffn_b_gate, L0_ffn_W1, L0_ffn_b1, L0_ffn_W2, L0_ffn_b2)
    x = x + _L0_attn_ref(_layernorm(x, axis=-1), L0_attn_norm_w, L0_attn_Wq, L0_attn_bq, L0_attn_Wk, L0_attn_bk, L0_attn_Wv, L0_attn_bv, L0_attn_Wo, L0_attn_bo)
    x = x + 0.5 * _L0_ffn_ref(_layernorm(x, axis=-1), L0_ffn_w_gate, L0_ffn_b_gate, L0_ffn_W1, L0_ffn_b1, L0_ffn_W2, L0_ffn_b2)
    return x

_drawn_inputs = setup_inputs


def setup_inputs(seed=0):
    import zlib

    import numpy as np

    out = dict(_drawn_inputs(seed))
    spreads = {'L0_attn_norm_w': (1.0, 0.2),
     'L0_attn_bq': (0.0, 0.8),
     'L0_attn_bk': (0.0, 0.8),
     'L0_attn_bv': (0.0, 0.1),
     'L0_attn_bo': (0.0, 0.1),
     'L0_ffn_b1': (0.0, 0.8),
     'L0_ffn_b2': (0.0, 0.424)}
    factors = {'L0_ffn_b_gate': 6.653}
    for name, (base, spread) in spreads.items():
        noise = np.random.default_rng([zlib.crc32(name.encode()), seed]).standard_normal(out[name].shape)
        drawn = base * np.exp(spread * noise) if base else spread * noise
        out[name] = jnp.asarray(drawn.astype(out[name].dtype))
    for name, factor in factors.items():
        out[name] = (out[name] * factor).astype(out[name].dtype)
    return out
```

```python
from contextlib import ExitStack

import numpy as np
import concourse.bass as bass
from concourse import mybir

F32 = mybir.dt.float32
BF16 = mybir.dt.bfloat16
I32 = mybir.dt.int32
U32 = mybir.dt.uint32
ALU = mybir.AluOpType
ACT = mybir.ActivationFunctionType
AX = mybir.AxisListType

P = 128
D = 128
B, T = 8, 256
NT = B * T // P
NQ = NT // 4
NE, HID = 8, 512
HC = HID // P
NS = NT + NE - 1
WCOLS = HID + HC * D + HC
NH, HD = 16, 8
NPAIR = NH // 2
BLK = 6
SROWS = 112
MROW = SROWS
KROWS = MROW + 3
LN_EPS, RMS_EPS = 1e-5, 1e-6
NEG = -1e30
SCALE = 1.0 / float(np.sqrt(np.float32(HD)))

C_ID, C_UP, C_MS, C_MT, C_ONE, C_J, C_REV, C_T = 0, 128, 256, 384, 512, 640, 656, 664
C_MHALF = C_T + NS
C_END = C_MHALF + NT


def constants():
    c = np.zeros((P, C_END), np.float32)
    i = np.arange(P)
    c[:, C_ID:C_ID + P] = np.eye(P)
    c[:, C_UP:C_UP + P] = i[:, None] < i[None, :]
    c[:, C_MS:C_MS + P] = np.where(i[None, :] > i[:, None], NEG, 0)
    c[:, C_MT:C_MT + P] = np.where(i[:, None] > i[None, :], NEG, 0)
    c[:, C_ONE:C_ONE + P] = 1
    c[:, C_J:C_J + NT] = P * np.arange(NT)
    c[:, C_REV:C_REV + NE] = NE - np.arange(NE)
    c[:, C_T:C_T + NS] = np.arange(NS)
    c[:, C_MHALF:C_END] = -0.5
    return c


def build(nc, x_in, wqkvo, bqk, rows_in, w_gate, experts, b2_in, const_in, out):
    ctx = ExitStack()
    with ctx:
        def sb(name, shape, dt=F32):
            return ctx.enter_context(nc.sbuf_tensor(name, shape, dt))

        def sem(name):
            return ctx.enter_context(nc.semaphore(name))

        def sems(name, n):
            return [sem(f"{name}{i}") for i in range(n)]

        bank = [ctx.enter_context(nc.psum_tensor(f"bank{i}", [P, 512], F32)) for i in range(8)]

        x = sb("x", [P, NT, D])
        xn = sb("xn", [P, NT, D])
        cst = sb("cst", [P, C_END])
        cb = sb("cb", [P, C_J], BF16)
        wt = sb("wt", [P, 4, D])
        bqk_sb = sb("bqk_sb", [P, 2])
        rows = sb("rows", [P, 4 * D])
        wg = sb("wg", [D, NE])
        ident = cst[:, C_ID:C_ID + P]
        ident_b = cb[:, C_ID:C_ID + P]
        norm_w, bv, bo = (rows[:, i * D:(i + 1) * D] for i in range(3))
        b_gate = rows[:, 3 * D:3 * D + NE]

        st6 = sb("st6", [P, NT, 6])
        mv = sb("mv", [P, NT, 2])
        tmp16 = sb("tmp16", [P, NT])
        rs = sb("rs", [P, NT])
        rr = sb("rr", [P, NT])

        gT = sb("gT", [P, 2, 512])
        lg = sb("lg", [P, NT, NE])
        sh = sb("sh", [P, NT, NE])
        ex = sb("ex", [P, NT, NE])
        mx = sb("mx", [P, NT])
        den = sb("den", [P, NT])
        pr = sb("pr", [P, NT])
        oh = sb("oh", [P, NT, NE])
        pick = sb("pick", [P, NT, NE])
        best = sb("best", [P, NT])
        onehot = sb("onehot", [P, NT, NE], BF16)
        before = sb("before", [P, NE, NT])
        keep = sb("keep", [P, NE, NT])
        base = sb("base", [P, NE, NT])
        cnt = sb("cnt", [P, NE])
        gtj = sb("gtj", [P, NE, NT])
        ntl = sb("ntl", [P, NE])
        endt = sb("endt", [P, NE])
        begt = sb("begt", [P, NE])
        ones8 = sb("ones8", [P, NE])
        slotb = sb("slotb", [P, NE, NT])
        slotm = sb("slotm", [P, NT, NE])
        slotf = sb("slotf", [P, NT])
        slot = sb("slot", [P, NT], U32)
        geq = sb("geq", [P, NS, NE])
        tef = sb("tef", [P, NS])
        te = sb("te", [P, NS], I32)

        zero = sb("zero", [P, 1024])
        xs_sb = sb("xs_sb", [P, 4, D])
        ew = sb("ew", [P, 4, WCOLS])
        eb2 = sb("eb2", [P, 4, D])
        xsT = sb("xsT", [P, 2, P])
        hT = sb("hT", [P, 2, HC, P])
        ys_sb = sb("ys_sb", [P, 4, D])
        yg = sb("yg", [P, NT, D])

        xb = sb("xb", [P, 2, 2, D])
        xbT = sb("xbT", [P, 2, T])
        qk = sb("qk", [P, 2, 2, T])
        qkr = sb("qkr", [P, 2, 2, T])
        spl = sb("spl", [P, 2, 3, 2, T], BF16)
        v = sb("v", [P, NT, D])
        va = sb("va", [P, 2, 2, NH, 32])
        qz = [sb(f"qz{i}", [P, NPAIR, 2, T], BF16) for i in range(2)]
        ks = [sb(f"ks{i}", [P, NPAIR, T], BF16) for i in range(2)]
        mh = sb("mh", [P, 2, 2, 8])
        mr = sb("mr", [P, 2, 2, 8])
        mb = sb("mb", [P, 2, 2, 3, 8], BF16)
        mT = sb("mT", [24, 2, T], BF16)
        pT = sb("pT", [P, 4, 512])
        oT = [sb(f"oT{i}", [P, 2, T]) for i in range(2)]
        rl = sb("rl", [P, 2, NPAIR, 2])
        an = sb("an", [P, 2, D])
        anT = sb("anT", [P, T])

        xs_d = nc.dram_tensor("xs_d", [NS * P, D], F32, kind="Internal").ap()
        ys_d = nc.dram_tensor("ys_d", [NS * P, D], F32, kind="Internal").ap()
        sp_d = nc.dram_tensor("sp_d", [B * 2 * 2 * BLK * HD * NPAIR, T], BF16, kind="Internal").ap()
        m_d = nc.dram_tensor("m_d", [B * 2, 24, T], BF16, kind="Internal").ap()

        x_in_s = sems("x_loaded", NQ)
        cst_s = sem("const_loaded")
        gate_s = sem("gate_loaded")
        attw_s = sem("attn_weights_loaded")
        zero_s = sem("zero_set")
        cb_s = sem("const_bf16")
        xs0_s = sem("sorted_zeroed")
        static_s = sem("static_buffers_set")
        final_s = sems("out_written", NQ)
        ln_st = sems("ln_stats", 3)
        ln_mv = sems("ln_meanvar", 3)
        ln_t = sems("ln_pool_chain", 3)
        ln_rs = sems("ln_scale", 3)
        ln_xn = sems("ln_normalised", 3)
        g_T = sems("gate_transposed", 2)
        g_Tc = sems("gate_transpose_copied", 2)
        g_lg = sems("gate_logits", 2)
        r_ch = sems("route_chain", 2)
        r_sh = sems("route_shifted", 2)
        r_ex = sems("route_exp", 2)
        r_oh = sems("route_onehot", 2)
        r_cnt = sems("route_counts", 2)
        r_slot = sems("route_slots", 2)
        scat = sems("scattered", 2)
        e_w = [sems(f"expert_weights{f}_", 4) for f in range(2)]
        e_xs = [sems(f"sorted_tile{f}_", 4) for f in range(2)]
        e_T = sems("sorted_transposed", 2)
        e_Tc = sems("sorted_transpose_copied", 2)
        e_h = sems("hidden_product", 2)
        e_ha = sems("hidden_relu_act", 2)
        e_hd = sems("hidden_relu_dve", 2)
        e_y = sems("out_product", 2)
        e_yc = sems("out_copied", 2)
        e_st = [sems(f"out_stored{f}_", 4) for f in range(2)]
        gath = [sems(f"gathered{f}_", NQ) for f in range(2)]
        comb = sems("combined", 2)

        q_xb = sem("seq_xn")
        q_res = sem("seq_residual")
        q_T = sem("seq_transposed")
        q_Tc = sem("seq_transpose_copied")
        q_qk = sem("seq_qk_product")
        q_v = sem("seq_v_product")
        q_qkc = sem("seq_qk_copied")
        q_s1 = sem("seq_split1")
        q_vc = sem("seq_v_copied")
        q_ch = sem("seq_split_chain")
        q_spl = sem("seq_split_done")
        q_std = sems("seq_split_stored", 2)
        a_va = sem("attn_v_spread")
        a_stk = [sems(f"stack_loaded{i}_", 2) for i in range(2)]
        a_s = sem("scores_q")
        a_mx = sem("scores_max")
        a_mch = sem("max_split_chain")
        a_mb = sem("max_split")
        a_mt = sem("max_transposed")
        a_mtc = sem("max_transpose_copied")
        a_md = sem("max_stored")
        a_m = sems("max_rows_loaded", 2)
        a_st = sem("scores_k")
        a_e = sem("exp_done")
        a_pv = sem("pv_done")
        a_ot = sem("attn_out_copied")
        a_oT = sem("attn_out_transposed")
        a_rl = sem("attn_recip")
        a_an = sem("attn_normalised")
        a_aT = sem("attn_norm_transposed")
        a_aTc = sem("attn_norm_transpose_copied")
        a_wo = sem("attn_projected")
        a_x = sem("attn_added")

        def need(eng, s, n):
            if not isinstance(n, int) or n > 0:
                eng.wait_ge(s, n)

        MM_BANK = dict(skip_group_check=True)
        block = ctx.enter_context(nc.Block())
        sp_rows = HD * NPAIR

        def sp_view(r0, t, j):
            return sp_d[bass.ds(r0 + (2 * t + j) * BLK * sp_rows, BLK * sp_rows), :]

        @block.sync
        def _(sp):
            xv = x_in.rearrange("(t p) d -> p t d", p=P)
            for q in range(NQ):
                sp.dma_start(x[:, 4 * q:4 * q + 4, :], xv[:, 4 * q:4 * q + 4, :]).then_inc(x_in_s[q], 16)
            sp.dma_start(cst[:, :], const_in).then_inc(cst_s, 16)
            sp.dma_start(wg[:, :], w_gate).then_inc(gate_s, 16)
            sp.dma_start(rows[:, :], rows_in.partition_broadcast(P)).then_inc(gate_s, 16)
            sp.dma_start(wt[:, :, :], wqkvo).then_inc(attw_s, 16)
            sp.dma_start(bqk_sb[:, :], bqk).then_inc(attw_s, 16)
            sp.wait_ge(zero_s, 1)
            xz = xs_d.rearrange("(p r) d -> p (r d)", p=P)
            for c in range(0, NS * D, 1024):
                w = min(1024, NS * D - c)
                sp.dma_start(xz[:, c:c + w], zero[:, 0:w]).then_inc(xs0_s, 16)

            def expert_loads(f):
                def load(t, i, k):
                    e = sp.value_load(te[0:1, bass.ds(t, 1)], min_val=0, max_val=NE - 1)
                    need(sp, e_y[f], t - 3)
                    need(sp, e_yc[f], t - 3)
                    sp.dma_start(ew[:, k, :], experts[bass.ds(e * P, P), :]).then_inc(e_w[f][k], 16)
                    sp.dma_start(eb2[:, k, :], b2_in[bass.ds(e * P, P), :]).then_inc(e_w[f][k], 16)
                    need(sp, e_T[f], t - 3)
                    sp.dma_start(xs_sb[:, k, :], xs_d[bass.ds(t * P, P), :]).then_inc(e_xs[f][k], 16)
                sp.wait_ge(r_slot[f], 2)
                sp.wait_ge(scat[f], 16 * NT)
                for k in range(4):
                    load(k, 0, k)
                with sp.Fori(1, NS // 4) as i:
                    for k in range(4):
                        load(4 * i + k, i, k)
                for k in range(NS % 4):
                    load(NS // 4 * 4 + k, NS // 4, k)

            def seq_stores(b, bh, k):
                r0 = b * (4 * BLK * sp_rows) if isinstance(b, int) else sp.snap(b * (4 * BLK * sp_rows))
                sp.wait_ge(q_spl, b + 1)
                for t, plan in ((0, ((0, 3, 0, 0), (3, 2, 1, 0), (5, 1, 2, 0))),
                                (1, ((0, 3, 0, 1), (3, 2, 0, 1), (5, 1, 0, 1)))):
                    for j in range(2):
                        dst = sp_view(r0, t, j).rearrange("(c r) n -> r c n", c=BLK)
                        for c0, n, s0, step in plan:
                            src = spl[64 * j:64 * j + 64, k, s0:s0 + (n if step else 1), t, :]
                            if not step:
                                src = src.broadcast_to((64, n, T))
                            sp.dma_start(dst[:, c0:c0 + n, :], src).then_inc(q_std[k], 16)

            def stack_load(b, bh, k, half):
                r0 = b * (4 * BLK * sp_rows) if isinstance(b, int) else sp.snap(b * (4 * BLK * sp_rows))
                need(sp, a_st, 12 * (b - 2) + 6 * half + 6)
                for j in range(2):
                    for t, buf in ((0, qz[k][64 * j:64 * j + 48, 4 * half:4 * half + 4, j, :]),
                                   (1, ks[k][64 * j:64 * j + 48, 4 * half:4 * half + 4, :])):
                        src = sp_view(r0, t, j).rearrange("(c pr) n -> c pr n", pr=NPAIR)
                        sp.dma_start(buf, src[:, 4 * half:4 * half + 4, :]).then_inc(a_stk[k][half], 16)

            def max_rows(b, k, half):
                n = 2 * b + half if isinstance(b, int) else sp.snap(2 * b + half)
                sp.wait_ge(a_mtc, n + 1)
                sp.dma_start(m_d[bass.ds(n, 1), :, :].rearrange("a r n -> (a r) n"),
                             mT[:, half, :]).then_inc(a_md, 16)
                sp.wait_ge(a_md, 16 * (n + 1))
                src = m_d[bass.ds(n, 1), :, :].rearrange("a (s r) n -> (a s) (r n)", s=3)
                sp.dma_start(qz[k][MROW:MROW + 3, 4 * half:4 * half + 4, :, :], src
                             ).then_inc(a_m[half], 16)

            expert_loads(0)
            sp.wait_ge(static_s, 8)
            with sp.Fori(0, B // 2) as i:
                for k in range(2):
                    seq_stores(2 * i + k, i, k)
            for k in range(2):
                sp.wait_ge(q_std[k], 192 * (B // 2))
            for half in range(2):
                stack_load(0, 0, 0, half)
            for half in range(2):
                stack_load(1, 0, 1, half)

            def step(b, bh, k, half, more):
                if half == 0:
                    max_rows(b, k, 1)
                elif more >= 1:
                    max_rows(b + 1, 1 - k, 0)
                if more >= 2:
                    stack_load(b + 2, bh + 1, k, half)
            max_rows(0, 0, 0)
            for half in range(2):
                step(0, 0, 0, half, 2)
            with sp.Fori(0, 2) as i:
                for half in range(2):
                    step(2 * i + 1, i, 1, half, 2)
                for half in range(2):
                    step(2 * i + 2, i + 1, 0, half, 2)
            for b, more in ((5, 2), (6, 1), (7, 0)):
                for half in range(2):
                    step(b, b // 2, b % 2, half, more)
            expert_loads(1)
            ov = out.rearrange("(t p) d -> p t d", p=P)
            for q in range(NQ):
                sp.wait_ge(comb[1], q + 1)
                sp.dma_start(ov[:, 4 * q:4 * q + 4, :], x[:, 4 * q:4 * q + 4, :]).then_inc(final_s[q], 16)
            for q in range(NQ):
                sp.wait_ge(final_s[q], 16)

        @block.gpsimd
        def _(pool):
            pool.memset(zero[:, :], 0.0).then_inc(zero_s, 1)
            for k in range(2):
                pool.memset(qz[k][:, :, :, :], 0.0).then_inc(static_s, 1)
                pool.memset(ks[k][:, :, :], 0.0).then_inc(static_s, 1)
            pool.memset(va[:, :, :, :, :], 0.0).then_inc(static_s, 1)
            pool.wait_ge(static_s, 5)
            for k in range(2):
                pool.memset(ks[k][96:128, :, :], -1.0).then_inc(static_s, 1)
                pool.wait_ge(static_s, 6 + k)
            pool.memset(va[:, :, :, :, HD:HD + 1], 1.0).then_inc(static_s, 1)

            def layernorm_scale(n):
                pool.wait_ge(ln_mv[n], NQ)
                pool.wait_ge(cst_s, 16)
                mh_ = cst[:, C_MHALF:C_END]
                pool.tensor_scalar(tmp16[:, :], mv[:, :, 1], LN_EPS, None, ALU.add).then_inc(ln_t[n], 1)
                pool.wait_ge(ln_t[n], 1)
                i1 = pool.tensor_tensor(rs[:, :], tmp16[:, :], mh_, ALU.pow)
                if n != 1:
                    i1.then_inc(ln_rs[n], 1)
                    return
                i1.then_inc(ln_t[n], 1)
                pool.wait_ge(ln_t[n], 2)
                pool.tensor_tensor(tmp16[:, :], mv[:, :, 1], rs[:, :], ALU.mult).then_inc(ln_t[n], 1)
                pool.wait_ge(ln_t[n], 3)
                pool.tensor_tensor(rr[:, :], tmp16[:, :], rs[:, :], ALU.mult).then_inc(ln_t[n], 1)
                pool.wait_ge(ln_t[n], 4)
                pool.tensor_scalar(tmp16[:, :], rr[:, :], RMS_EPS, None, ALU.add).then_inc(ln_t[n], 1)
                pool.wait_ge(ln_t[n], 5)
                pool.tensor_tensor(rr[:, :], tmp16[:, :], mh_, ALU.pow).then_inc(ln_t[n], 1)
                pool.wait_ge(ln_t[n], 6)
                pool.tensor_tensor(rr[:, :], rr[:, :], rs[:, :], ALU.mult).then_inc(ln_rs[n], 1)

            def scatter(f):
                pool.wait_ge(r_slot[f], 1)
                if f == 0:
                    pool.wait_ge(xs0_s, 16 * -(-NS * D // 1024))
                for t in range(NT):
                    pool.indirect_dma_start(xs_d[:, :], bass.IndirectOffsetOnAxis(ap=slot[:, t:t + 1], axis=0),
                                            xn[:, t, :], None).then_inc(scat[f], 16)

            def gather(f):
                for k in range(4):
                    pool.wait_ge(e_st[f][k], 16 * ((NS - k + 3) // 4))
                for t in range(NT):
                    pool.indirect_dma_start(yg[:, t, :], None, ys_d[:, :],
                                            bass.IndirectOffsetOnAxis(ap=slot[:, t:t + 1], axis=0)
                                            ).then_inc(gath[f][t // 4], 16)

            layernorm_scale(0)
            scatter(0)
            gather(0)
            layernorm_scale(1)

            def seq_xn(b, k):
                need(pool, q_T, b - 1)
                tiles = bass.ds(2 * b, 2)
                nw = norm_w.unsqueeze(1).broadcast_to((P, 2, D))
                pool.tensor_tensor(xb[:, k, :, :], xn[:, tiles, :], nw, ALU.mult).then_inc(q_xb, 1)
                pool.wait_ge(q_xb, b + 1)
                pool.tensor_tensor(x[:, tiles, :], x[:, tiles, :], xb[:, k, :, :], ALU.add).then_inc(q_res, 1)
                pool.wait_ge(q_res, 2 * b + 1)
                pool.tensor_tensor(x[:, tiles, :], x[:, tiles, :],
                                   bo.unsqueeze(1).broadcast_to((P, 2, D)), ALU.add).then_inc(q_res, 1)
            pool.wait_ge(ln_xn[1], NQ)
            for b in range(B):
                seq_xn(b, b % 2)

            def max_split(b, half):
                n = 2 * b + half
                pool.wait_ge(a_mx, 6 * n + 6)
                need(pool, a_mt, n - 1)
                z_ = zero[:, 0:16].rearrange("p (q h) -> p q h", q=2)
                m_, r_, s_ = mh[:, half, :, :], mr[:, half, :, :], mb[:, half, :, :, :]
                pool.tensor_tensor(s_[:, :, 0, :], m_, z_, ALU.add).then_inc(a_mch, 1)
                pool.wait_ge(a_mch, 4 * n + 1)
                pool.tensor_tensor(r_, m_, s_[:, :, 0, :], ALU.subtract).then_inc(a_mch, 1)
                pool.wait_ge(a_mch, 4 * n + 2)
                pool.tensor_tensor(s_[:, :, 1, :], r_, z_, ALU.add).then_inc(a_mch, 1)
                pool.wait_ge(a_mch, 4 * n + 3)
                pool.tensor_tensor(r_, r_, s_[:, :, 1, :], ALU.subtract).then_inc(a_mch, 1)
                pool.wait_ge(a_mch, 4 * n + 4)
                pool.tensor_tensor(s_[:, :, 2, :], r_, z_, ALU.add).then_inc(a_mb, 1)
            max_split(0, 0)
            max_split(0, 1)

            for half in range(2):
                max_split(1, half)
            with pool.Fori(1, 4) as i:
                for k in range(2):
                    for half in range(2):
                        max_split(2 * i + k, half)
            layernorm_scale(2)
            scatter(1)
            gather(1)

        @block.scalar
        def _(act):
            def gate_copies(f):
                for q in range(NQ):
                    act.wait_ge(g_T[f], q + 1)
                    if q >= 2:
                        act.wait_ge(g_lg[f], q - 1)
                    act.copy(gT[:, q % 2, :], bank[q % 2][:, :]).then_inc(g_Tc[f], 1)
                act.wait_ge(r_sh[f], 1)
                act.activation(ex[:, :, :], sh[:, :, :], ACT.Exp).then_inc(r_ex[f], 1)

            def expert_tiles(f):
                def copy_T(t, par):
                    act.wait_ge(e_T[f], t + 1)
                    need(act, e_h[f], t - 1)
                    act.copy(xsT[:, par, :], bank[par][:, 0:P]).then_inc(e_Tc[f], 1)

                def relu(t, par, k):
                    act.wait_ge(e_h[f], t + 1)
                    need(act, e_y[f], t - 1)
                    for c in range(2):
                        mm = act.activation(hT[:, par, c, :], bank[2 + 2 * par][:, c * P:(c + 1) * P], ACT.Relu,
                                            bias=ew[:, k, HID + HC * D + c:HID + HC * D + c + 1])
                    mm.then_inc(e_ha[f], 1)

                def store(t, k):
                    act.wait_ge(e_yc[f], t + 1)
                    act.dma_start(ys_d[bass.ds(t * P, P), :], ys_sb[:, k, :]).then_inc(e_st[f][k], 16)

                def step(t, k, do_T=True, do_h=True, do_s=True):
                    if do_T:
                        copy_T(t + 2, k % 2)
                    if do_h:
                        relu(t + 1, (k + 1) % 2, (k + 1) % 4)
                    if do_s:
                        store(t - 1, (k + 3) % 4)
                copy_T(0, 0)
                copy_T(1, 1)
                relu(0, 0, 0)
                for k in range(4):
                    step(k, k, do_s=k > 0)
                with act.Fori(1, NS // 4) as i:
                    for k in range(4):
                        step(4 * i + k, k)
                for t in range(NS // 4 * 4, NS):
                    step(t, t % 4, do_T=t + 2 < NS, do_h=t + 1 < NS)
                store(NS - 1, (NS - 1) % 4)

            gate_copies(0)
            expert_tiles(0)

            act.wait_ge(attw_s, 32)

            def seq_split1(b, bh, k):
                need(act, q_std[k], 192 * bh)
                act.copy(spl[:, k, 0, :, :], qk[:, k, :, :]).then_inc(q_s1, 1)

            def seq(b, bh, k):
                act.wait_ge(q_T, b + 1)
                need(act, q_v, b - 1)
                act.copy(xbT[:, k, :], bank[k][:, 0:T]).then_inc(q_Tc, 1)
                act.wait_ge(q_qk, b + 1)
                need(act, q_spl, b - 1)
                for t in range(2):
                    mm = act.activation(qk[:, k, t, :], bank[2 + k][:, t * T:(t + 1) * T], ACT.Identity,
                                        bias=bqk_sb[:, t:t + 1])
                mm.then_inc(q_qkc, 1)
                act.wait_ge(q_qkc, b + 1)
                seq_split1(b, bh, k)
            for k in range(2):
                seq(k, 0, k)
            with act.Fori(1, B // 2) as i:
                for k in range(2):
                    seq(2 * i + k, i, k)

            def exp_unit(b, half, u):
                n = 12 * b + 6 * half + u
                act.wait_ge(a_st, n + 1)
                need(act, a_pv, n - 3)
                act.activation(pT[:, (6 * half + u) % 4, :], bank[2 + u % 2][:, :], ACT.Exp, scale=SCALE
                               ).then_inc(a_e, 1)

            def max_copy(b, half):
                act.wait_ge(a_mt, 2 * b + half + 1)
                need(act, a_md, 16 * (2 * b + half - 1))
                act.copy(mT[:, half, :], bank[6][0:24, 0:P].bitcast(BF16)).then_inc(a_mtc, 1)

            def out_copy(b, half):
                act.wait_ge(a_pv, 12 * b + 6 * half + 6)
                need(act, a_oT, 2 * b)
                act.copy(oT[half][:, :, :], bank[4 + half][:, :].rearrange("p (g n) -> p g n", g=2)
                         ).then_inc(a_ot, 1)

            def step(b, half, more, first=False):
                for u in range(6):
                    exp_unit(b, half, u)
                    if u == 0 and not (first and half == 0):
                        out_copy(b if half else b - 1, 1 - half)
                    if u == 1:
                        if half == 0:
                            max_copy(b, 1)
                        elif more:
                            max_copy(b + 1, 0)
                    if u == 5 and half == 0 and not first:
                        act.wait_ge(a_aT, b)
                        act.copy(anT[:, :], bank[7][:, 0:T]).then_inc(a_aTc, 1)
            max_copy(0, 0)
            for half in range(2):
                step(0, half, True, first=True)
            with act.Fori(0, 3) as i:
                for k in range(2):
                    for half in range(2):
                        step(2 * i + 1 + k, half, True)
            for half in range(2):
                step(7, half, False)
            out_copy(7, 1)
            act.wait_ge(a_aT, B)
            act.copy(anT[:, :], bank[7][:, 0:T]).then_inc(a_aTc, 1)

            gate_copies(1)
            expert_tiles(1)

        @block.vector
        def _(dve):
            dve.wait_ge(cst_s, 16)
            dve.tensor_copy(cb[:, :], cst[:, 0:C_J]).then_inc(cb_s, 1)
            dve.memset(keep[:, :, :], 1.0).then_inc(cb_s, 1)
            dve.memset(before[:, :, 0:1], 0.0)
            dve.memset(ones8[:, :], 1.0).then_inc(cb_s, 1)
            dve.wait_ge(cb_s, 3)
            dve.memset(keep[:, :, 0:1], 0.0).then_inc(cb_s, 1)

            def layernorm(n, scale):
                for q in range(NQ):
                    if n == 0:
                        dve.wait_ge(x_in_s[q], 16)
                    elif n == 1:
                        dve.wait_ge(comb[0], q + 1)
                    for t in range(4 * q, 4 * q + 4):
                        i1 = dve.bn_stats(st6[:, t, :], x[:, t, :])
                    i1.then_inc(ln_st[n], 1)
                    dve.wait_ge(ln_st[n], q + 1)
                    for t in range(4 * q, 4 * q + 4):
                        i1 = dve.bn_aggr(mv[:, t, :], st6[:, t, :])
                    i1.then_inc(ln_mv[n], 1)
                dve.wait_ge(ln_rs[n], 1)
                for q in range(NQ):
                    for t in range(4 * q, 4 * q + 4):
                        i1 = dve.tensor_scalar(xn[:, t, :], x[:, t, :], mv[:, t, 0:1], scale[:, t:t + 1],
                                               ALU.subtract, ALU.mult)
                    i1.then_inc(ln_xn[n], 1)

            def route(f):
                for q in range(NQ):
                    dve.wait_ge(g_lg[f], q + 1)
                    i1 = dve.tensor_tensor(lg[:, 4 * q:4 * q + 4, :],
                                           bank[2 + q][:, 0:4 * NE].rearrange("p (t e) -> p t e", t=4),
                                           b_gate.unsqueeze(1).broadcast_to((P, 4, NE)), ALU.add)
                n = [0]

                def chain(ins):
                    n[0] += 1
                    ins.then_inc(r_ch[f], 1)
                    dve.wait_ge(r_ch[f], n[0])
                chain(i1)
                chain(dve.tensor_reduce(mx[:, :], lg[:, :, :], AX.X, ALU.max))
                mxb = mx[:, :].unsqueeze(2).broadcast_to((P, NT, NE))
                dve.tensor_tensor(sh[:, :, :], lg[:, :, :], mxb, ALU.subtract).then_inc(r_sh[f], 1)
                chain(dve.tensor_tensor(oh[:, :, :], lg[:, :, :], mxb, ALU.is_equal))
                chain(dve.tensor_tensor(pick[:, :, :], oh[:, :, :],
                                        cst[:, C_REV:C_REV + NE].unsqueeze(1).broadcast_to((P, NT, NE)), ALU.mult))
                chain(dve.tensor_reduce(best[:, :], pick[:, :, :], AX.X, ALU.max))
                dve.tensor_tensor(onehot[:, :, :], pick[:, :, :],
                                  best[:, :].unsqueeze(2).broadcast_to((P, NT, NE)), ALU.is_equal
                                  ).then_inc(r_oh[f], 1)
                dve.wait_ge(r_ex[f], 1)
                chain(dve.tensor_reduce(den[:, :], ex[:, :, :], AX.X, ALU.add))
                chain(dve.reciprocal(mx[:, :], den[:, :]))
                chain(dve.tensor_scalar(pr[:, :], mx[:, :], 0.5, None, ALU.mult))
                dve.wait_ge(r_cnt[f], 1)
                inside = bank[6][:, 0:P].rearrange("p (t e) -> p t e", t=NT)
                total = bank[6][:, P:2 * P].rearrange("p (t e) -> p e t", t=NT)
                chain(dve.tensor_copy(before[:, :, 1:NT], total[:, :, 0:NT - 1]))
                chain(dve.tensor_tensor_scan(base[:, :, :].rearrange("p e t -> p (e t)"),
                                             keep[:, :, :].rearrange("p e t -> p (e t)"),
                                             before[:, :, :].rearrange("p e t -> p (e t)"),
                                             0.0, ALU.mult, ALU.add))
                chain(dve.tensor_tensor(cnt[:, :], base[:, :, NT - 1], total[:, :, NT - 1], ALU.add))
                chain(dve.tensor_tensor(gtj[:, :, :], cnt[:, :].unsqueeze(2).broadcast_to((P, NE, NT)),
                                        cst[:, C_J:C_J + NT].unsqueeze(1).broadcast_to((P, NE, NT)), ALU.is_gt))
                chain(dve.tensor_reduce(ntl[:, :], gtj[:, :, :], AX.X, ALU.add))
                chain(dve.tensor_tensor_scan(endt[:, :], ones8[:, :], ntl[:, :], 0.0, ALU.mult, ALU.add))
                chain(dve.tensor_tensor(begt[:, :], endt[:, :], ntl[:, :], ALU.subtract))
                chain(dve.scalar_tensor_tensor(slotb[:, :, :], begt[:, :].unsqueeze(2).broadcast_to((P, NE, NT)),
                                               float(P), base[:, :, :], ALU.mult, ALU.add))
                chain(dve.tensor_tensor(slotm[:, :, :], inside,
                                        slotb[:, :, :].rearrange("p e t -> p t e"), ALU.add))
                chain(dve.tensor_tensor(slotm[:, :, :], slotm[:, :, :], onehot[:, :, :], ALU.mult))
                chain(dve.tensor_reduce(slotf[:, :], slotm[:, :, :], AX.X, ALU.add))
                dve.tensor_copy(slot[:, :], slotf[:, :]).then_inc(r_slot[f], 1)
                chain(dve.tensor_tensor(geq[:, :, :], cst[:, C_T:C_T + NS].unsqueeze(2).broadcast_to((P, NS, NE)),
                                        endt[:, :].unsqueeze(1).broadcast_to((P, NS, NE)), ALU.is_ge))
                chain(dve.tensor_reduce(tef[:, :], geq[:, :, :], AX.X, ALU.add))
                dve.tensor_scalar(te[:, :], tef[:, :], float(NE - 1), None, ALU.min).then_inc(r_slot[f], 1)

            def expert_tiles(f):
                def relu(t, par, k):
                    dve.wait_ge(e_h[f], t + 1)
                    need(dve, e_y[f], t - 1)
                    for c in range(2, HC):
                        i1 = dve.tensor_scalar(hT[:, par, c, :], bank[3 + 2 * par][:, (c - 2) * P:(c - 1) * P],
                                               ew[:, k, HID + HC * D + c:HID + HC * D + c + 1], 0.0,
                                               ALU.add, ALU.max)
                    i1.then_inc(e_hd[f], 1)

                def out_copy(t, i, k):
                    dve.wait_ge(e_y[f], t + 1)
                    need(dve, e_st[f][k], 16 * i)
                    dve.tensor_tensor(ys_sb[:, k, :], bank[6 + k % 2][:, 0:D], eb2[:, k, :], ALU.add
                                      ).then_inc(e_yc[f], 1)

                def step(t, i, k, do_h=True):
                    if do_h:
                        relu(t + 1, (k + 1) % 2, (k + 1) % 4)
                    out_copy(t, i, k)
                relu(0, 0, 0)
                for k in range(4):
                    step(k, 0, k)
                with dve.Fori(1, NS // 4) as i:
                    for k in range(4):
                        step(4 * i + k, i, k)
                for t in range(NS // 4 * 4, NS):
                    step(t, NS // 4, t % 4, do_h=t + 1 < NS)

            def combine(f):
                for q in range(NQ):
                    dve.wait_ge(gath[f][q], 64)
                    for t in range(4 * q, 4 * q + 4):
                        i1 = dve.scalar_tensor_tensor(x[:, t, :], yg[:, t, :], pr[:, t:t + 1], x[:, t, :],
                                                      ALU.mult, ALU.add)
                    i1.then_inc(comb[f], 1)

            layernorm(0, rs)
            dve.wait_ge(gate_s, 32)
            route(0)
            expert_tiles(0)
            combine(0)
            layernorm(1, rr)

            def seq(b, bh, k):
                dve.wait_ge(q_v, b + 1)
                dve.tensor_tensor(v[:, bass.ds(2 * b, 2), :],
                                  bank[4 + k][:, 0:2 * D].rearrange("p (t d) -> p t d", t=2),
                                  bv.unsqueeze(1).broadcast_to((P, 2, D)), ALU.add).then_inc(q_vc, 1)
                dve.wait_ge(q_s1, b + 1)
                dve.tensor_tensor(qkr[:, k, :, :], qk[:, k, :, :], spl[:, k, 0, :, :], ALU.subtract
                                  ).then_inc(q_ch, 1)
                dve.wait_ge(q_ch, 2 * b + 1)
                dve.tensor_copy(spl[:, k, 1, :, :], qkr[:, k, :, :]).then_inc(q_ch, 1)
                dve.wait_ge(q_ch, 2 * b + 2)
                dve.tensor_tensor(spl[:, k, 2, :, :], qkr[:, k, :, :], spl[:, k, 1, :, :], ALU.subtract
                                  ).then_inc(q_spl, 1)
            for k in range(2):
                seq(k, 0, k)
            with dve.Fori(1, B // 2) as i:
                for k in range(2):
                    seq(2 * i + k, i, k)

            def max_unit(b, half, u):
                dve.wait_ge(a_s, 12 * b + 6 * half + u + 1)
                pp, w = divmod(u, 3)
                if u == 0:
                    need(dve, a_mb, 2 * b + half - 1)
                if w < 2:
                    dve.tensor_reduce(mh[:, half, 1, 4 * pp + 2 * w:4 * pp + 2 * w + 2],
                                      bank[u % 2][:, :].rearrange("p (h n) -> p h n", h=2), AX.X, ALU.max
                                      ).then_inc(a_mx, 1)
                else:
                    dve.tensor_reduce(mh[:, half, 0, 4 * pp:4 * pp + 4],
                                      bank[u % 2][:, :].rearrange("p (h n) -> p h n", h=4), AX.X, ALU.max
                                      ).then_inc(a_mx, 1)

            def v_spread(b, k):
                need(dve, a_pv, 12 * (b - 1))
                dve.tensor_scalar(va[:, k, :, :, 0:HD], v[:, bass.ds(2 * b, 2), :].rearrange(
                    "p t (h d) -> p t h d", h=NH), 1.0, None, ALU.mult).then_inc(a_va, 1)

            def normalise(b, qt):
                dve.wait_ge(a_oT, 2 * b + qt + 1)
                o = bank[7 - qt][:, :].rearrange("p (g j c) -> p g j c", g=NPAIR, j=2)
                dve.reciprocal(rl[:, qt, :, :], o[:, :, :, HD]).then_inc(a_rl, 1)
                dve.wait_ge(a_rl, 2 * b + qt + 1)
                dve.tensor_tensor(an[:, qt, :].rearrange("p (j g d) -> p g j d", j=2, g=NPAIR), o[:, :, :, 0:HD],
                                  rl[:, qt, :, :].unsqueeze(3).broadcast_to((P, NPAIR, 2, HD)), ALU.mult
                                  ).then_inc(a_an, 1)

            def add_out(b):
                dve.wait_ge(a_wo, b + 1)
                dve.tensor_tensor(x[:, bass.ds(2 * b, 2), :],
                                  bank[7][:, 0:2 * D].rearrange("p (t d) -> p t d", t=2),
                                  x[:, bass.ds(2 * b, 2), :], ALU.add).then_inc(a_x, 1)

            def step(b, k, half, more, first=False):
                for u in range(6):
                    if more:
                        max_unit(b + 1, half, u)
                    if more and half == 0 and u == 2:
                        v_spread(b + 1, 1 - k)
                    if half == 0 and not first:
                        if u == 3:
                            normalise(b - 1, 0)
                        if u == 4:
                            normalise(b - 1, 1)
                    if half == 1 and not first and u == 4:
                        add_out(b - 1)
            dve.wait_ge(q_res, 2 * B)
            dve.wait_ge(q_vc, B)
            dve.wait_ge(static_s, 8)
            v_spread(0, 0)
            for half in range(2):
                for u in range(6):
                    max_unit(0, half, u)
            for half in range(2):
                step(0, 0, half, True, first=True)
            with dve.Fori(0, 3) as i:
                for k in range(2):
                    for half in range(2):
                        step(2 * i + 1 + k, 1 - k, half, True)
            for half in range(2):
                step(7, 1, half, False)
            normalise(7, 0)
            normalise(7, 1)
            add_out(7)
            dve.wait_ge(a_x, B)
            layernorm(2, rs)
            route(1)
            expert_tiles(1)
            combine(1)

        @block.tensor
        def _(pe):
            pe.wait_ge(cst_s, 16)

            def gate(f):
                def logits(q):
                    pe.wait_ge(g_Tc[f], q + 1)
                    for t in range(4):
                        mm = pe.matmul(bank[2 + q][:, t * NE:(t + 1) * NE], gT[:, q % 2, t * P:(t + 1) * P], wg[:, :],
                                       start=True, stop=True)
                    mm.then_inc(g_lg[f], 1)
                for q in range(NQ):
                    pe.wait_ge(ln_xn[2 * f], q + 1)
                    if q >= 2:
                        pe.wait_ge(g_Tc[f], q - 1)
                    for t in range(4):
                        mm = pe.transpose(bank[q % 2][:, t * P:(t + 1) * P], xn[:, 4 * q + t, :], ident)
                    mm.then_inc(g_T[f], 1)
                    if q == 1 and f == 0:
                        pe.wait_ge(gate_s, 32)
                    if q >= 1:
                        logits(q - 1)
                logits(NQ - 1)
                pe.wait_ge(r_oh[f], 1)
                oh_ = onehot[:, :, :].rearrange("p t e -> p (t e)")
                pe.matmul(bank[6][:, 0:P], cb[:, C_UP:C_UP + P], oh_, start=True, stop=True)
                pe.matmul(bank[6][:, P:2 * P], cb[:, C_ONE:C_ONE + P], oh_, start=True, stop=True
                          ).then_inc(r_cnt[f], 1)

            def expert_tiles(f):
                def turn(t, i, k):
                    pe.wait_ge(e_xs[f][k], 16 * (i + 1))
                    need(pe, e_Tc[f], t - 1)
                    pe.transpose(bank[k % 2][:, 0:P], xs_sb[:, k, :], ident).then_inc(e_T[f], 1)

                def hidden(t, i, k):
                    pe.wait_ge(e_Tc[f], t + 1)
                    pe.wait_ge(e_w[f][k], 32 * (i + 1))
                    need(pe, e_ha[f], t - 1)
                    need(pe, e_hd[f], t - 1)
                    for c in range(HC):
                        mm = pe.matmul(bank[2 + 2 * (k % 2) + c // 2][:, (c % 2) * P:(c % 2 + 1) * P],
                                       ew[:, k, c * P:(c + 1) * P], xsT[:, k % 2, :], start=True, stop=True)
                    mm.then_inc(e_h[f], 1)

                def output(t, k):
                    pe.wait_ge(e_ha[f], t + 1)
                    pe.wait_ge(e_hd[f], t + 1)
                    need(pe, e_yc[f], t - 1)
                    for c in range(HC):
                        mm = pe.matmul(bank[6 + k % 2][:, 0:D], hT[:, k % 2, c, :],
                                       ew[:, k, HID + c * D:HID + (c + 1) * D], start=(c == 0), stop=(c == HC - 1))
                    mm.then_inc(e_y[f], 1)

                def step(t, i, k, do_T=True, do_h=True):
                    if do_T:
                        turn(t + 2, i + (k + 2) // 4, (k + 2) % 4)
                    if do_h:
                        hidden(t + 1, i + (k + 1) // 4, (k + 1) % 4)
                    output(t, k)
                turn(0, 0, 0)
                turn(1, 0, 1)
                hidden(0, 0, 0)
                for k in range(4):
                    step(k, 0, k)
                with pe.Fori(1, NS // 4) as i:
                    for k in range(4):
                        step(4 * i + k, i, k)
                for t in range(NS // 4 * 4, NS):
                    step(t, NS // 4, t % 4, do_T=t + 2 < NS, do_h=t + 1 < NS)

            pe.wait_ge(cb_s, 1)
            gate(0)
            expert_tiles(0)

            pe.wait_ge(attw_s, 32)

            def seq(b, k):
                pe.wait_ge(q_xb, b + 1)
                need(pe, q_Tc, b - 1)
                for t in range(2):
                    mm = pe.transpose(bank[k][:, t * P:(t + 1) * P], xb[:, k, t, :], ident)
                mm.then_inc(q_T, 1)
                pe.wait_ge(q_Tc, b + 1)
                need(pe, q_qkc, b - 1)
                for t in range(2):
                    mm = pe.matmul(bank[2 + k][:, t * T:(t + 1) * T], wt[:, t, :], xbT[:, k, :],
                                   start=True, stop=True)
                mm.then_inc(q_qk, 1)
                need(pe, q_vc, b - 1)
                for t in range(2):
                    mm = pe.matmul(bank[4 + k][:, t * D:(t + 1) * D], xbT[:, k, t * P:(t + 1) * P], wt[:, 2, :],
                                   start=True, stop=True)
                mm.then_inc(q_v, 1)
            for k in range(2):
                seq(k, k)
            with pe.Fori(1, B // 2) as i:
                for k in range(2):
                    seq(2 * i + k, k)
            pe.wait_ge(q_qkc, B)
            pe.wait_ge(q_vc, B)

            maskS = cb[:, C_MS:C_MS + P]
            maskT = cb[:, C_MT:C_MT + P]

            def scores_q(b, bh, k, half, u):
                pp, w = divmod(u, 3)
                if u == 0:
                    pe.wait_ge(a_stk[k][half], 64 * (bh + 1))
                need(pe, a_mx, 12 * b + 6 * half + u - 1)
                o = bank[u % 2]
                if w < 2:
                    pair = 4 * half + 2 * pp + w
                    ov = o[:, :].rearrange("p (j n) -> p j n", j=2)
                    pe.matmul(ov[:, :, P:T], ident_b, maskS.unsqueeze(1).broadcast_to((P, 2, P)),
                              start=True, stop=False, **MM_BANK)
                    for j in range(2):
                        mm = pe.matmul(ov[:, j, :], qz[k][0:SROWS, pair, j, P:T], ks[k][0:SROWS, pair, :],
                                       start=False, stop=True, **MM_BANK)
                else:
                    ov = o[:, :].rearrange("p (h n) -> p h n", h=4)
                    pe.matmul(ov, ident_b, maskS.unsqueeze(1).broadcast_to((P, 4, P)),
                              start=True, stop=False, **MM_BANK)
                    for h in range(4):
                        pair = 4 * half + 2 * pp + h // 2
                        mm = pe.matmul(ov[:, h, :], qz[k][0:SROWS, pair, h % 2, 0:P], ks[k][0:SROWS, pair, 0:P],
                                       start=False, stop=True, **MM_BANK)
                mm.then_inc(a_s, 1)

            def scores_k(b, k, half, u):
                pp, w = divmod(u, 3)
                if u == 0:
                    pe.wait_ge(a_m[half], 16 * (b + 1))
                need(pe, a_e, 12 * b + 6 * half + u - 1)
                o = bank[2 + u % 2]
                if w < 2:
                    pair = 4 * half + 2 * pp + w
                    ov = o[:, :].rearrange("p (j n) -> p j n", j=2)
                    pe.matmul(ov[:, :, 0:P], ident_b, maskT.unsqueeze(1).broadcast_to((P, 2, P)),
                              start=True, stop=False, **MM_BANK)
                    mm = pe.matmul(ov, ks[k][0:KROWS, pair, 0:P], qz[k][0:KROWS, pair, :, :],
                                   start=False, stop=True, **MM_BANK)
                else:
                    ov = o[:, :].rearrange("p (i j n) -> p i j n", i=2, j=2)
                    pe.matmul(o[:, :].rearrange("p (h n) -> p h n", h=4), ident_b,
                              maskT.unsqueeze(1).broadcast_to((P, 4, P)), start=True, stop=False, **MM_BANK)
                    for i in range(2):
                        pair = 4 * half + 2 * pp + i
                        mm = pe.matmul(ov[:, i, :, :], ks[k][0:KROWS, pair, P:T], qz[k][0:KROWS, pair, :, P:T],
                                       start=False, stop=True, **MM_BANK)
                mm.then_inc(a_st, 1)

            def pv(b, k, half, u):
                pp, w = divmod(u, 3)
                n = 12 * b + 6 * half + u
                pe.wait_ge(a_e, n + 1)
                if u == 0:
                    need(pe, a_ot, 2 * b + half - 1)
                    if half == 0:
                        pe.wait_ge(a_va, b + 1)
                o = bank[4 + half]
                p_ = pT[:, (6 * half + u) % 4, :]
                for h in range(4) if w == 2 else range(2 * w, 2 * w + 2):
                    pair, j = 4 * half + 2 * pp + h // 2, h % 2
                    if w < 2:
                        mm = pe.matmul(o[32 * h:32 * h + 32, pp * T:(pp + 1) * T], va[:, k, 0, 8 * j + pair, :],
                                       p_[:, j * T:(j + 1) * T], start=True, stop=False, **MM_BANK)
                    else:
                        mm = pe.matmul(o[32 * h:32 * h + 32, pp * T + P:(pp + 1) * T], va[:, k, 1, 8 * j + pair, :],
                                       p_[:, h * P:(h + 1) * P], start=False, stop=True, **MM_BANK)
                mm.then_inc(a_pv, 1)

            def turn_max(b, half):
                pe.wait_ge(a_mb, 2 * b + half + 1)
                o = bank[6][0:24, 0:P].bitcast(BF16)
                for qt in range(2):
                    mm = pe.transpose(o[:, qt * P:(qt + 1) * P],
                                      mb[:, half, qt, :, :].rearrange("p s h -> p (s h)"), ident_b)
                mm.then_inc(a_mt, 1)

            def turn_out(b, qt):
                pe.wait_ge(a_ot, 2 * b + 2)
                for g in range(4):
                    mm = pe.transpose(bank[7 - qt][:, g * P:(g + 1) * P], oT[g // 2][:, g % 2, qt * P:(qt + 1) * P],
                                      ident)
                mm.then_inc(a_oT, 1)

            def turn_norm(b):
                pe.wait_ge(a_an, 2 * b + 2)
                for qt in range(2):
                    mm = pe.transpose(bank[7][:, qt * P:(qt + 1) * P], an[:, qt, :], ident)
                mm.then_inc(a_aT, 1)

            def project(b):
                pe.wait_ge(a_aTc, b + 1)
                for qt in range(2):
                    mm = pe.matmul(bank[7][:, qt * D:(qt + 1) * D], anT[:, qt * P:(qt + 1) * P], wt[:, 3, :],
                                   start=True, stop=True)
                mm.then_inc(a_wo, 1)

            def step(b, bh, k, half, more, first=False):
                for u in range(6):
                    scores_k(b, k, half, u)
                    if more:
                        scores_q(b + 1, bh, 1 - k, half, u)
                    if u > 0:
                        pv(b, k, half, u - 1)
                    elif half:
                        pv(b, k, 0, 5)
                    elif not first:
                        pv(b - 1, 1 - k, 1, 5)
                    if u == 1:
                        if half == 0:
                            if not first:
                                pe.wait_ge(a_mtc, 2 * b + 1)
                            turn_max(b, 1)
                        elif more:
                            if not first:
                                pe.wait_ge(a_an, 2 * b)
                            pe.wait_ge(a_mtc, 2 * b + 2)
                            turn_max(b + 1, 0)
                    if half == 0 and not first:
                        if u == 2:
                            need(pe, a_x, b - 1)
                            turn_out(b - 1, 0)
                        if u == 3:
                            pe.wait_ge(a_mtc, 2 * b + 2)
                            turn_out(b - 1, 1)
                        if u == 5:
                            turn_norm(b - 1)
                    if half == 1 and not first and u == 3:
                        project(b - 1)
            for half in range(2):
                for u in range(6):
                    scores_q(0, 0, 0, half, u)
            turn_max(0, 0)
            pe.wait_ge(a_mtc, 1)
            for half in range(2):
                step(0, 0, 0, half, True, first=True)
            with pe.Fori(0, 3) as i:
                for half in range(2):
                    step(2 * i + 1, i + 1, 1, half, True)
                for half in range(2):
                    step(2 * i + 2, i + 1, 0, half, True)
            for half in range(2):
                step(7, 3, 1, half, False)
            pv(7, 1, 1, 5)
            pe.wait_ge(a_x, 7)
            turn_out(7, 0)
            turn_out(7, 1)
            turn_norm(7)
            project(7)
            gate(1)
            expert_tiles(1)


_INS = ["x", "wqkvo", "bqk", "rows", "w_gate", "experts", "b2", "const"]


def kernel(L0_attn_x, L0_attn_norm_w, L0_attn_Wq, L0_attn_bq, L0_attn_Wk, L0_attn_bk, L0_attn_Wv, L0_attn_bv,
           L0_attn_Wo, L0_attn_bo, L0_ffn_w_gate, L0_ffn_b_gate, L0_ffn_W1, L0_ffn_b1, L0_ffn_W2, L0_ffn_b2):
    import concourse.bacc as bacc
    from concourse.bass_utils import run_bass_kernel_spmd

    f = lambda a: np.asarray(a)
    perm = np.arange(D).reshape(2, NPAIR, HD).transpose(0, 2, 1).reshape(-1)
    wq, wk, wv, wo = (f(w).T for w in (L0_attn_Wq, L0_attn_Wk, L0_attn_Wv, L0_attn_Wo))
    pad = np.zeros(D - NE, f(L0_ffn_b_gate).dtype)
    w2 = f(L0_ffn_W2).reshape(NE, HC, P, D).transpose(0, 2, 1, 3).reshape(NE, P, HC * D)
    b1 = f(L0_ffn_b1).reshape(NE, HC, P).transpose(0, 2, 1)
    arrays = {
        "x": f(L0_attn_x).reshape(B * T, D),
        "wqkvo": np.stack([wq[:, perm], wk[:, perm], wv, wo], axis=1),
        "bqk": np.stack([f(L0_attn_bq)[perm], f(L0_attn_bk)[perm]], axis=1),
        "rows": np.concatenate([f(L0_attn_norm_w), f(L0_attn_bv), f(L0_attn_bo), f(L0_ffn_b_gate), pad]),
        "w_gate": f(L0_ffn_w_gate),
        "experts": np.concatenate([f(L0_ffn_W1), w2, b1], axis=2).reshape(NE * P, WCOLS),
        "b2": np.broadcast_to(f(L0_ffn_b2)[:, None, :], (NE, P, D)).reshape(NE * P, D),
        "const": constants(),
    }
    nc = bacc.Bacc("TRN2", target_bir_lowering=False, num_devices=1)
    arrays = {f"in_{n}": np.ascontiguousarray(arrays[n]) for n in _INS}
    args = [nc.dram_tensor(n, a.shape, mybir.dt.from_np(a.dtype), kind="ExternalInput").ap()
            for n, a in arrays.items()]
    out = nc.dram_tensor("out_0", (B * T, D), F32, kind="ExternalOutput").ap()
    build(nc, *args, out)
    r = run_bass_kernel_spmd(nc, [arrays], core_ids=[0])
    return r.results[0]["out_0"].reshape(B, T, D)
```

```python
from contextlib import ExitStack

import numpy as np
import concourse.bass as bass
from concourse import mybir

F32 = mybir.dt.float32
BF16 = mybir.dt.bfloat16
I32 = mybir.dt.int32
U32 = mybir.dt.uint32
ALU = mybir.AluOpType
ACT = mybir.ActivationFunctionType
AX = mybir.AxisListType

P = 128
D = 128
B, T = 8, 256
NT = B * T // P
NQ = NT // 4
NE, HID = 8, 512
HC = HID // P
NS = NT + NE - 1
WCOLS = HID + HC + D
ECOLS = WCOLS + HC * D
AHEAD = 5
NOTOK = NT * P
NH, HD = 16, 8
NPAIR = NH // 2
BLK = 6
SROWS = 112
MROW = SROWS
KROWS = MROW + 3
LN_EPS, RMS_EPS = 1e-5, 1e-6
NEG = -1e30
SCALE = 1.0 / float(np.sqrt(np.float32(HD)))

C_ID, C_UP, C_MS, C_MT, C_ONE, C_J, C_REV, C_T = 0, 128, 256, 384, 512, 640, 656, 664
C_MHALF = C_T + NS
C_PLACE = C_MHALF + 4
C_TOK = C_PLACE + P
C_SELF = C_TOK + NT
C_END = C_SELF + NS


def constants():
    c = np.zeros((P, C_END), np.float32)
    i = np.arange(P)
    c[:, C_ID:C_ID + P] = np.eye(P)
    c[:, C_UP:C_UP + P] = i[:, None] < i[None, :]
    c[:, C_MS:C_MS + P] = np.where(i[None, :] > i[:, None], NEG, 0)
    c[:, C_MT:C_MT + P] = np.where(i[:, None] > i[None, :], NEG, 0)
    c[:, C_ONE:C_ONE + P] = 1
    c[:, C_J:C_J + NT] = P * np.arange(NT)
    c[:, C_REV:C_REV + NE] = NE - np.arange(NE)
    c[:, C_T:C_T + NS] = np.arange(NS)
    c[:, C_MHALF:C_MHALF + 4] = -0.5
    c[:, C_PLACE:C_PLACE + P] = i
    c[:, C_TOK:C_TOK + NT] = P * np.arange(NT) + i[:, None] - NOTOK
    c[:, C_SELF:C_END] = NOTOK + P * np.arange(NS) + i[:, None]
    return c


def build(nc, x_in, wqkvo, bqk, rows_in, w_gate, experts_in, const_in, out):
    ctx = ExitStack()
    with ctx:
        def sb(name, shape, dt=F32):
            return ctx.enter_context(nc.sbuf_tensor(name, shape, dt))

        def sem(name):
            return ctx.enter_context(nc.semaphore(name))

        def sems(name, n):
            return [sem(f"{name}{i}") for i in range(n)]

        bank = [ctx.enter_context(nc.psum_tensor(f"bank{i}", [P, 512], F32)) for i in range(8)]

        x = sb("x", [P, NT, D])
        xn = sb("xn", [P, NT, D])
        cst = sb("cst", [P, C_END])
        cb = sb("cb", [P, C_J], BF16)
        wt = sb("wt", [P, 4, D])
        bqk_sb = sb("bqk_sb", [P, 2])
        rows = sb("rows", [P, 4 * D])
        experts = sb("experts", [P, NE, ECOLS])
        wg = sb("wg", [D, NE])
        ident = cst[:, C_ID:C_ID + P]
        ident_b = cb[:, C_ID:C_ID + P]
        norm_w, bv, bo = (rows[:, i * D:(i + 1) * D] for i in range(3))
        b_gate = rows[:, 3 * D:3 * D + NE]

        st6 = sb("st6", [P, NT, 6])
        mv = sb("mv", [P, NT, 2])
        vs = sb("vs", [P, NT])
        rs = sb("rs", [P, NT])

        gT = sb("gT", [P, 2, 512])
        lg = sb("lg", [P, NT, NE])
        sh = sb("sh", [P, NT, NE])
        ex = sb("ex", [P, NT, NE])
        mx = sb("mx", [P, NT])
        den = sb("den", [P, NT])
        pr = sb("pr", [P, NT])
        oh = sb("oh", [P, NT, NE])
        pick = sb("pick", [P, NT, NE])
        best = sb("best", [P, NT])
        onehot = sb("onehot", [P, NT, NE], BF16)
        before = sb("before", [P, NE, NT])
        keep = sb("keep", [P, NE, NT])
        base = sb("base", [P, NE, NT])
        cnt = sb("cnt", [P, NE])
        gtj = sb("gtj", [P, NE, NT])
        ntl = sb("ntl", [P, NE])
        endt = sb("endt", [P, NE])
        begt = sb("begt", [P, NE])
        ones8 = sb("ones8", [P, NE])
        slotb = sb("slotb", [P, NE, NT])
        slotm = sb("slotm", [P, NT, NE])
        slotf = sb("slotf", [P, NT])
        sloti = sb("sloti", [P, NT], I32)
        tilei = sb("tilei", [P, NT], I32)
        tilef = sb("tilef", [P, NT])
        lane = sb("lane", [P, NT])
        hot_tile = sb("hot_tile", [P, NT, NS])
        hot_lane = sb("hot_lane", [P, NT, P])
        tokm = sb("tokm", [P, NT])
        tokf = sb("tokf", [P, NS])
        tok_s = sb("tok_s", [P, NS], U32)
        tok_g = sb("tok_g", [P, NS], U32)
        geq = sb("geq", [P, NS, NE])
        tef = sb("tef", [P, NS])
        te = sb("te", [P, NS], I32)

        zero = sb("zero", [P, D])
        xs_sb = sb("xs_sb", [P, 4, D])
        ew = sb("ew", [P, 4, WCOLS])
        xsT = sb("xsT", [P, 2, P])
        hT = sb("hT", [P, 2, HC, P])
        ys_sb = sb("ys_sb", [P, 4, D])
        yg = sb("yg", [P, NT, D])

        xb = sb("xb", [P, 2, 2, D])
        xbT = sb("xbT", [P, 2, T])
        qk = sb("qk", [P, 2, 2, T])
        qkr = sb("qkr", [P, 2, 2, T])
        spl = sb("spl", [P, 2, 3, 2, T], BF16)
        v = sb("v", [P, NT, D])
        va = sb("va", [P, 2, 2, NH, 32])
        qz = [sb(f"qz{i}", [P, NPAIR, 2, T], BF16) for i in range(2)]
        ks = [sb(f"ks{i}", [P, NPAIR, T], BF16) for i in range(2)]
        mh = sb("mh", [P, 2, 2, 8])
        mr = sb("mr", [P, 2, 2, 8])
        mb = sb("mb", [P, 2, 2, 3, 8], BF16)
        mT = sb("mT", [24, 2, T], BF16)
        pT = sb("pT", [P, 4, 512])
        oT = [sb(f"oT{i}", [P, 2, T]) for i in range(2)]
        rl = sb("rl", [P, 2, NPAIR, 2])
        an = sb("an", [P, 2, D])
        anT = sb("anT", [P, T])

        xn_d = nc.dram_tensor("xn_d", [NOTOK + 1, D], F32, kind="Internal").ap()
        y_d = nc.dram_tensor("y_d", [NOTOK + NS * P, D], F32, kind="Internal").ap()
        sp_d = nc.dram_tensor("sp_d", [B * 2 * 2 * BLK * HD * NPAIR, T], BF16, kind="Internal").ap()
        m_d = nc.dram_tensor("m_d", [B * 2, 24, T], BF16, kind="Internal").ap()

        x_in_s = sems("x_loaded", NQ)
        cst_s = sem("const_loaded")
        gate_s = sem("gate_loaded")
        attw_s = sem("attn_weights_loaded")
        zero_s = sem("zero_set")
        cb_s = sem("const_bf16")
        notok_s = sem("no_token_row_zeroed")
        static_s = sem("static_buffers_set")
        final_s = sems("out_written", NQ)
        ln_st = sems("ln_stats", 3)
        ln_mv = sems("ln_meanvar", 3)
        ln_vs = sems("ln_shifted_var", 3)
        ln_rs = sems("ln_scale", 3)
        ln_xn = sems("ln_normalised", 3)
        g_T = sems("gate_transposed", 2)
        g_Tc = sems("gate_transpose_copied", 2)
        g_lg = sems("gate_logits", 2)
        r_ch = sems("route_chain", 2)
        r_sh = sems("route_shifted", 2)
        r_ex = sems("route_exp", 2)
        r_oh = sems("route_onehot", 2)
        r_cnt = sems("route_counts", 2)
        r_te = sems("route_tile_experts", 2)
        r_hi = sems("route_hot_tile", 2)
        r_lo = sems("route_hot_lane", 2)
        r_inv = sems("route_inverse", 2)
        r_tok = sems("route_tokens", 2)
        xn_st = sems("xn_stored", 2)
        e_all = sem("experts_loaded")
        e_w = sems("expert_weights_copied", 2)
        e_xs = [sems(f"tile_gathered{f}_", 4) for f in range(2)]
        e_T = sems("sorted_transposed", 2)
        e_Tc = sems("sorted_transpose_copied", 2)
        e_h = sems("hidden_product", 2)
        e_ha = sems("hidden_relu_act", 2)
        e_hd = sems("hidden_relu_dve", 2)
        e_y = sems("out_product", 2)
        e_yc = sems("out_copied", 2)
        e_st = [sems(f"out_scattered{f}_", 4) for f in range(2)]
        y_ld = [sems(f"y_loaded{f}_", NQ) for f in range(2)]
        comb = sems("combined", 2)

        q_xb = sem("seq_xn")
        q_res = sem("seq_residual")
        q_T = sem("seq_transposed")
        q_Tc = sem("seq_transpose_copied")
        q_qk = sem("seq_qk_product")
        q_v = sem("seq_v_product")
        q_qkc = sem("seq_qk_copied")
        q_s1 = sem("seq_split1")
        q_vc = sem("seq_v_copied")
        q_ch = sem("seq_split_chain")
        q_spl = sem("seq_split_done")
        q_std = sems("seq_split_stored", 2)
        a_va = sem("attn_v_spread")
        a_stk = [sems(f"stack_loaded{i}_", 2) for i in range(2)]
        a_s = sem("scores_q")
        a_mx = sem("scores_max")
        a_mch = sem("max_split_chain")
        a_mb = sem("max_split")
        a_mt = sem("max_transposed")
        a_mtc = sem("max_transpose_copied")
        a_md = sem("max_stored")
        a_m = sems("max_rows_loaded", 2)
        a_st = sem("scores_k")
        a_e = sem("exp_done")
        a_pv = sem("pv_done")
        a_ot = sem("attn_out_copied")
        a_oT = sem("attn_out_transposed")
        a_rl = sem("attn_recip")
        a_an = sem("attn_normalised")
        a_aT = sem("attn_norm_transposed")
        a_aTc = sem("attn_norm_transpose_copied")
        a_wo = sem("attn_projected")
        a_x = sem("attn_added")

        def need(eng, s, n):
            if not isinstance(n, int) or n > 0:
                eng.wait_ge(s, n)

        MM_BANK = dict(skip_group_check=True)
        block = ctx.enter_context(nc.Block())
        sp_rows = HD * NPAIR

        def sp_view(r0, t, j):
            return sp_d[bass.ds(r0 + (2 * t + j) * BLK * sp_rows, BLK * sp_rows), :]

        @block.sync
        def _(sp):
            xv = x_in.rearrange("(t p) d -> p t d", p=P)
            for q in range(NQ):
                sp.dma_start(x[:, 4 * q:4 * q + 4, :], xv[:, 4 * q:4 * q + 4, :]).then_inc(x_in_s[q], 16)
            sp.dma_start(cst[:, :], const_in).then_inc(cst_s, 16)
            sp.dma_start(wg[:, :], w_gate).then_inc(gate_s, 16)
            sp.dma_start(rows[:, :], rows_in.partition_broadcast(P)).then_inc(gate_s, 16)
            sp.dma_start(wt[:, :, :], wqkvo).then_inc(attw_s, 16)
            sp.dma_start(bqk_sb[:, :], bqk).then_inc(attw_s, 16)
            for e in range(NE):
                sp.dma_start(experts[:, e, :], experts_in[e * P:(e + 1) * P, :]).then_inc(e_all, 16)
            sp.wait_ge(zero_s, 1)
            sp.dma_start(xn_d[NOTOK:NOTOK + 1, :], zero[0:1, :]).then_inc(notok_s, 16)

            def tok_view(dram, q):
                return dram[4 * q * P:4 * (q + 1) * P, :].rearrange("(t p) d -> p t d", p=P)

            def xn_stores(f):
                for q in range(NQ):
                    sp.wait_ge(ln_xn[2 * f], q + 1)
                    sp.dma_start(tok_view(xn_d, q), xn[:, 4 * q:4 * q + 4, :]).then_inc(xn_st[f], 16)

            def y_loads(f):
                for k in range(4):
                    sp.wait_ge(e_st[f][k], 16 * ((NS - k + 3) // 4))
                for q in range(NQ):
                    sp.dma_start(yg[:, 4 * q:4 * q + 4, :], tok_view(y_d, q)).then_inc(y_ld[f][q], 16)

            def seq_stores(b, bh, k):
                r0 = b * (4 * BLK * sp_rows) if isinstance(b, int) else sp.snap(b * (4 * BLK * sp_rows))
                sp.wait_ge(q_spl, b + 1)
                for t, plan in ((0, ((0, 3, 0, 0), (3, 2, 1, 0), (5, 1, 2, 0))),
                                (1, ((0, 3, 0, 1), (3, 2, 0, 1), (5, 1, 0, 1)))):
                    for j in range(2):
                        dst = sp_view(r0, t, j).rearrange("(c r) n -> r c n", c=BLK)
                        for c0, n, s0, step in plan:
                            src = spl[64 * j:64 * j + 64, k, s0:s0 + (n if step else 1), t, :]
                            if not step:
                                src = src.broadcast_to((64, n, T))
                            sp.dma_start(dst[:, c0:c0 + n, :], src).then_inc(q_std[k], 16)

            def stack_load(b, bh, k, half):
                r0 = b * (4 * BLK * sp_rows) if isinstance(b, int) else sp.snap(b * (4 * BLK * sp_rows))
                need(sp, a_st, 12 * (b - 2) + 6 * half + 6)
                for j in range(2):
                    for t, buf in ((0, qz[k][64 * j:64 * j + 48, 4 * half:4 * half + 4, j, :]),
                                   (1, ks[k][64 * j:64 * j + 48, 4 * half:4 * half + 4, :])):
                        src = sp_view(r0, t, j).rearrange("(c pr) n -> c pr n", pr=NPAIR)
                        sp.dma_start(buf, src[:, 4 * half:4 * half + 4, :]).then_inc(a_stk[k][half], 16)

            def max_rows(b, k, half):
                n = 2 * b + half if isinstance(b, int) else sp.snap(2 * b + half)
                sp.wait_ge(a_mtc, n + 1)
                sp.dma_start(m_d[bass.ds(n, 1), :, :].rearrange("a r n -> (a r) n"),
                             mT[:, half, :]).then_inc(a_md, 16)
                sp.wait_ge(a_md, 16 * (n + 1))
                src = m_d[bass.ds(n, 1), :, :].rearrange("a (s r) n -> (a s) (r n)", s=3)
                sp.dma_start(qz[k][MROW:MROW + 3, 4 * half:4 * half + 4, :, :], src
                             ).then_inc(a_m[half], 16)

            xn_stores(0)
            y_loads(0)
            sp.wait_ge(static_s, 8)
            with sp.Fori(0, B // 2) as i:
                for k in range(2):
                    seq_stores(2 * i + k, i, k)
            for k in range(2):
                sp.wait_ge(q_std[k], 192 * (B // 2))
            for half in range(2):
                stack_load(0, 0, 0, half)
            for half in range(2):
                stack_load(1, 0, 1, half)

            def step(b, bh, k, half, more):
                if half == 0:
                    max_rows(b, k, 1)
                elif more >= 1:
                    max_rows(b + 1, 1 - k, 0)
                if more >= 2:
                    stack_load(b + 2, bh + 1, k, half)
            max_rows(0, 0, 0)
            for half in range(2):
                step(0, 0, 0, half, 2)
            with sp.Fori(0, 2) as i:
                for half in range(2):
                    step(2 * i + 1, i, 1, half, 2)
                for half in range(2):
                    step(2 * i + 2, i + 1, 0, half, 2)
            for b, more in ((5, 2), (6, 1), (7, 0)):
                for half in range(2):
                    step(b, b // 2, b % 2, half, more)
            xn_stores(1)
            y_loads(1)
            ov = out.rearrange("(t p) d -> p t d", p=P)
            for q in range(NQ):
                sp.wait_ge(comb[1], q + 1)
                sp.dma_start(ov[:, 4 * q:4 * q + 4, :], x[:, 4 * q:4 * q + 4, :]).then_inc(final_s[q], 16)
            for q in range(NQ):
                sp.wait_ge(final_s[q], 16)

        @block.gpsimd
        def _(pool):
            pool.memset(zero[:, :], 0.0).then_inc(zero_s, 1)
            def ln_scale(n, q):
                tiles = slice(4 * q, 4 * q + 4)
                mul, add = (1.0 + RMS_EPS, RMS_EPS * LN_EPS) if n == 1 else (1.0, LN_EPS)
                pool.wait_ge(ln_mv[n], q + 1)
                pool.tensor_scalar(vs[:, tiles], mv[:, tiles, 1], mul, add, ALU.mult, ALU.add
                                   ).then_inc(ln_vs[n], 1)
                pool.wait_ge(ln_vs[n], q + 1)
                pool.tensor_tensor(rs[:, tiles], vs[:, tiles], cst[:, C_MHALF:C_MHALF + 4], ALU.pow
                                   ).then_inc(ln_rs[n], 1)

            def expert_tiles(f):
                def gather(t):
                    need(pool, e_T[f], t - 3)
                    pool.indirect_dma_start(xs_sb[:, t % 4, :], None, xn_d[:, :],
                                            bass.IndirectOffsetOnAxis(ap=tok_g[:, t:t + 1], axis=0)
                                            ).then_inc(e_xs[f][t % 4], 16)

                def scatter(t):
                    pool.wait_ge(e_yc[f], t + 1)
                    pool.indirect_dma_start(y_d[:, :], bass.IndirectOffsetOnAxis(ap=tok_s[:, t:t + 1], axis=0),
                                            ys_sb[:, t % 4, :], None).then_inc(e_st[f][t % 4], 16)

                pool.wait_ge(xn_st[f], 16 * NQ)
                if f == 0:
                    pool.wait_ge(notok_s, 16)
                pool.wait_ge(r_tok[f], 2)
                for t in range(AHEAD):
                    gather(t)
                for t in range(NS):
                    if t + AHEAD < NS:
                        gather(t + AHEAD)
                    scatter(t)

            pool.wait_ge(cst_s, 16)
            for q in range(NQ):
                ln_scale(0, q)
            for k in range(2):
                pool.memset(qz[k][:, :, :, :], 0.0).then_inc(static_s, 1)
                pool.memset(ks[k][:, :, :], 0.0).then_inc(static_s, 1)
            pool.memset(va[:, :, :, :, :], 0.0).then_inc(static_s, 1)
            pool.wait_ge(static_s, 5)
            for k in range(2):
                pool.memset(ks[k][96:128, :, :], -1.0).then_inc(static_s, 1)
                pool.wait_ge(static_s, 6 + k)
            pool.memset(va[:, :, :, :, HD:HD + 1], 1.0).then_inc(static_s, 1)
            expert_tiles(0)
            for q in range(NQ):
                ln_scale(1, q)

            def seq_xn(b, k):
                need(pool, q_T, b - 1)
                tiles = bass.ds(2 * b, 2)
                nw = norm_w.unsqueeze(1).broadcast_to((P, 2, D))
                pool.tensor_tensor(xb[:, k, :, :], xn[:, tiles, :], nw, ALU.mult).then_inc(q_xb, 1)
                pool.wait_ge(q_xb, b + 1)
                pool.tensor_tensor(x[:, tiles, :], x[:, tiles, :], xb[:, k, :, :], ALU.add).then_inc(q_res, 1)
                pool.wait_ge(q_res, 2 * b + 1)
                pool.tensor_tensor(x[:, tiles, :], x[:, tiles, :],
                                   bo.unsqueeze(1).broadcast_to((P, 2, D)), ALU.add).then_inc(q_res, 1)
            pool.wait_ge(ln_xn[1], NQ)
            for b in range(B):
                seq_xn(b, b % 2)

            def max_split(b, half):
                n = 2 * b + half
                pool.wait_ge(a_mx, 6 * n + 6)
                need(pool, a_mt, n - 1)
                z_ = zero[:, 0:16].rearrange("p (q h) -> p q h", q=2)
                m_, r_, s_ = mh[:, half, :, :], mr[:, half, :, :], mb[:, half, :, :, :]
                pool.tensor_tensor(s_[:, :, 0, :], m_, z_, ALU.add).then_inc(a_mch, 1)
                pool.wait_ge(a_mch, 4 * n + 1)
                pool.tensor_tensor(r_, m_, s_[:, :, 0, :], ALU.subtract).then_inc(a_mch, 1)
                pool.wait_ge(a_mch, 4 * n + 2)
                pool.tensor_tensor(s_[:, :, 1, :], r_, z_, ALU.add).then_inc(a_mch, 1)
                pool.wait_ge(a_mch, 4 * n + 3)
                pool.tensor_tensor(r_, r_, s_[:, :, 1, :], ALU.subtract).then_inc(a_mch, 1)
                pool.wait_ge(a_mch, 4 * n + 4)
                pool.tensor_tensor(s_[:, :, 2, :], r_, z_, ALU.add).then_inc(a_mb, 1)
            max_split(0, 0)
            max_split(0, 1)

            for half in range(2):
                max_split(1, half)
            with pool.Fori(1, 4) as i:
                for k in range(2):
                    for half in range(2):
                        max_split(2 * i + k, half)
            for q in range(NQ):
                ln_scale(2, q)
            expert_tiles(1)

        @block.scalar
        def _(act):
            def gate_copies(f):
                for q in range(NQ):
                    act.wait_ge(g_T[f], q + 1)
                    if q >= 2:
                        act.wait_ge(g_lg[f], q - 1)
                    act.copy(gT[:, q % 2, :], bank[q % 2][:, :]).then_inc(g_Tc[f], 1)
                act.wait_ge(r_sh[f], 1)
                act.activation(ex[:, :, :], sh[:, :, :], ACT.Exp).then_inc(r_ex[f], 1)

            def expert_tiles(f):
                def copy_T(t, par):
                    act.wait_ge(e_T[f], t + 1)
                    need(act, e_h[f], t - 1)
                    act.copy(xsT[:, par, :], bank[par][:, 0:P]).then_inc(e_Tc[f], 1)

                def relu(t, par, k):
                    act.wait_ge(e_h[f], t + 1)
                    need(act, e_y[f], t - 1)
                    for c in range(2):
                        mm = act.activation(hT[:, par, c, :], bank[2 + 2 * par][:, c * P:(c + 1) * P], ACT.Relu,
                                            bias=ew[:, k, HID + c:HID + c + 1])
                    mm.then_inc(e_ha[f], 1)

                def step(t, k, do_T=True, do_h=True):
                    if do_T:
                        copy_T(t + 2, k % 2)
                    if do_h:
                        relu(t + 1, (k + 1) % 2, (k + 1) % 4)
                copy_T(0, 0)
                copy_T(1, 1)
                relu(0, 0, 0)
                for k in range(4):
                    step(k, k)
                with act.Fori(1, NS // 4) as i:
                    for k in range(4):
                        step(4 * i + k, k)
                for t in range(NS // 4 * 4, NS):
                    step(t, t % 4, do_T=t + 2 < NS, do_h=t + 1 < NS)

            gate_copies(0)
            expert_tiles(0)

            act.wait_ge(attw_s, 32)

            def seq_split1(b, bh, k):
                need(act, q_std[k], 192 * bh)
                act.copy(spl[:, k, 0, :, :], qk[:, k, :, :]).then_inc(q_s1, 1)

            def seq(b, bh, k):
                act.wait_ge(q_T, b + 1)
                need(act, q_v, b - 1)
                act.copy(xbT[:, k, :], bank[k][:, 0:T]).then_inc(q_Tc, 1)
                act.wait_ge(q_qk, b + 1)
                need(act, q_spl, b - 1)
                for t in range(2):
                    mm = act.activation(qk[:, k, t, :], bank[2 + k][:, t * T:(t + 1) * T], ACT.Identity,
                                        bias=bqk_sb[:, t:t + 1])
                mm.then_inc(q_qkc, 1)
                act.wait_ge(q_qkc, b + 1)
                seq_split1(b, bh, k)
            for k in range(2):
                seq(k, 0, k)
            with act.Fori(1, B // 2) as i:
                for k in range(2):
                    seq(2 * i + k, i, k)

            def exp_unit(b, half, u):
                n = 12 * b + 6 * half + u
                act.wait_ge(a_st, n + 1)
                need(act, a_pv, n - 3)
                act.activation(pT[:, (6 * half + u) % 4, :], bank[2 + u % 2][:, :], ACT.Exp, scale=SCALE
                               ).then_inc(a_e, 1)

            def max_copy(b, half):
                act.wait_ge(a_mt, 2 * b + half + 1)
                need(act, a_md, 16 * (2 * b + half - 1))
                act.copy(mT[:, half, :], bank[6][0:24, 0:P].bitcast(BF16)).then_inc(a_mtc, 1)

            def out_copy(b, half):
                act.wait_ge(a_pv, 12 * b + 6 * half + 6)
                need(act, a_oT, 2 * b)
                act.copy(oT[half][:, :, :], bank[4 + half][:, :].rearrange("p (g n) -> p g n", g=2)
                         ).then_inc(a_ot, 1)

            def step(b, half, more, first=False):
                for u in range(6):
                    exp_unit(b, half, u)
                    if u == 0 and not (first and half == 0):
                        out_copy(b if half else b - 1, 1 - half)
                    if u == 1:
                        if half == 0:
                            max_copy(b, 1)
                        elif more:
                            max_copy(b + 1, 0)
                    if u == 5 and half == 0 and not first:
                        act.wait_ge(a_aT, b)
                        act.copy(anT[:, :], bank[7][:, 0:T]).then_inc(a_aTc, 1)
            max_copy(0, 0)
            for half in range(2):
                step(0, half, True, first=True)
            with act.Fori(0, 3) as i:
                for k in range(2):
                    for half in range(2):
                        step(2 * i + 1 + k, half, True)
            for half in range(2):
                step(7, half, False)
            out_copy(7, 1)
            act.wait_ge(a_aT, B)
            act.copy(anT[:, :], bank[7][:, 0:T]).then_inc(a_aTc, 1)

            gate_copies(1)
            expert_tiles(1)

        @block.vector
        def _(dve):
            dve.wait_ge(cst_s, 16)
            dve.tensor_copy(cb[:, :], cst[:, 0:C_J]).then_inc(cb_s, 1)
            dve.memset(keep[:, :, :], 1.0).then_inc(cb_s, 1)
            dve.memset(before[:, :, 0:1], 0.0)
            dve.memset(ones8[:, :], 1.0).then_inc(cb_s, 1)
            dve.wait_ge(cb_s, 3)
            dve.memset(keep[:, :, 0:1], 0.0).then_inc(cb_s, 1)

            def ln_stats(n, q):
                if n == 0:
                    dve.wait_ge(x_in_s[q], 16)
                elif n == 1:
                    dve.wait_ge(comb[0], q + 1)
                for t in range(4 * q, 4 * q + 4):
                    i1 = dve.bn_stats(st6[:, t, :], x[:, t, :])
                i1.then_inc(ln_st[n], 1)
                dve.wait_ge(ln_st[n], q + 1)
                for t in range(4 * q, 4 * q + 4):
                    i1 = dve.bn_aggr(mv[:, t, :], st6[:, t, :])
                i1.then_inc(ln_mv[n], 1)

            def ln_apply(n, q):
                dve.wait_ge(ln_rs[n], q + 1)
                for t in range(4 * q, 4 * q + 4):
                    i1 = dve.tensor_scalar(xn[:, t, :], x[:, t, :], mv[:, t, 0:1], rs[:, t:t + 1],
                                           ALU.subtract, ALU.mult)
                i1.then_inc(ln_xn[n], 1)

            def layernorm(n):
                for q in range(NQ):
                    if n == 1:
                        combine(0, q)
                    ln_stats(n, q)
                    if q == 0:
                        continue
                    ln_apply(n, q - 1)
                ln_apply(n, NQ - 1)

            def route(f):
                for q in range(NQ):
                    dve.wait_ge(g_lg[f], q + 1)
                    i1 = dve.tensor_tensor(lg[:, 4 * q:4 * q + 4, :],
                                           bank[2 + q][:, 0:4 * NE].rearrange("p (t e) -> p t e", t=4),
                                           b_gate.unsqueeze(1).broadcast_to((P, 4, NE)), ALU.add)
                n = [0]

                def chain(ins):
                    n[0] += 1
                    ins.then_inc(r_ch[f], 1)
                    dve.wait_ge(r_ch[f], n[0])
                chain(i1)
                chain(dve.tensor_reduce(mx[:, :], lg[:, :, :], AX.X, ALU.max))
                mxb = mx[:, :].unsqueeze(2).broadcast_to((P, NT, NE))
                dve.tensor_tensor(sh[:, :, :], lg[:, :, :], mxb, ALU.subtract).then_inc(r_sh[f], 1)
                chain(dve.tensor_tensor(oh[:, :, :], lg[:, :, :], mxb, ALU.is_equal))
                chain(dve.tensor_tensor(pick[:, :, :], oh[:, :, :],
                                        cst[:, C_REV:C_REV + NE].unsqueeze(1).broadcast_to((P, NT, NE)), ALU.mult))
                chain(dve.tensor_reduce(best[:, :], pick[:, :, :], AX.X, ALU.max))
                dve.tensor_tensor(onehot[:, :, :], pick[:, :, :],
                                  best[:, :].unsqueeze(2).broadcast_to((P, NT, NE)), ALU.is_equal
                                  ).then_inc(r_oh[f], 1)
                dve.wait_ge(r_ex[f], 1)
                chain(dve.tensor_reduce(den[:, :], ex[:, :, :], AX.X, ALU.add))
                chain(dve.reciprocal(mx[:, :], den[:, :]))
                chain(dve.tensor_scalar(pr[:, :], mx[:, :], 0.5, None, ALU.mult))
                dve.wait_ge(r_cnt[f], 1)
                inside = bank[6][:, 0:P].rearrange("p (t e) -> p t e", t=NT)
                total = bank[6][:, P:2 * P].rearrange("p (t e) -> p e t", t=NT)
                chain(dve.tensor_copy(before[:, :, 1:NT], total[:, :, 0:NT - 1]))
                chain(dve.tensor_tensor_scan(base[:, :, :].rearrange("p e t -> p (e t)"),
                                             keep[:, :, :].rearrange("p e t -> p (e t)"),
                                             before[:, :, :].rearrange("p e t -> p (e t)"),
                                             0.0, ALU.mult, ALU.add))
                chain(dve.tensor_tensor(cnt[:, :], base[:, :, NT - 1], total[:, :, NT - 1], ALU.add))
                chain(dve.tensor_tensor(gtj[:, :, :], cnt[:, :].unsqueeze(2).broadcast_to((P, NE, NT)),
                                        cst[:, C_J:C_J + NT].unsqueeze(1).broadcast_to((P, NE, NT)), ALU.is_gt))
                chain(dve.tensor_reduce(ntl[:, :], gtj[:, :, :], AX.X, ALU.add))
                chain(dve.tensor_tensor_scan(endt[:, :], ones8[:, :], ntl[:, :], 0.0, ALU.mult, ALU.add))
                chain(dve.tensor_tensor(begt[:, :], endt[:, :], ntl[:, :], ALU.subtract))
                chain(dve.scalar_tensor_tensor(slotb[:, :, :], begt[:, :].unsqueeze(2).broadcast_to((P, NE, NT)),
                                               float(P), base[:, :, :], ALU.mult, ALU.add))
                chain(dve.tensor_tensor(slotm[:, :, :], inside,
                                        slotb[:, :, :].rearrange("p e t -> p t e"), ALU.add))
                chain(dve.tensor_tensor(slotm[:, :, :], slotm[:, :, :], onehot[:, :, :], ALU.mult))
                chain(dve.tensor_reduce(slotf[:, :], slotm[:, :, :], AX.X, ALU.add))
                chain(dve.tensor_copy(sloti[:, :], slotf[:, :]))
                chain(dve.tensor_scalar(tilei[:, :], sloti[:, :], 7, None, ALU.logical_shift_right))
                chain(dve.tensor_copy(tilef[:, :], tilei[:, :]))
                chain(dve.scalar_tensor_tensor(lane[:, :], tilef[:, :], -float(P), slotf[:, :], ALU.mult, ALU.add))
                chain(dve.tensor_tensor(tokm[:, :], cst[:, C_TOK:C_TOK + NT], slotf[:, :], ALU.subtract))
                chain(dve.tensor_tensor(hot_tile[:, :, :], tilef[:, :].unsqueeze(2).broadcast_to((P, NT, NS)),
                                        cst[:, C_T:C_T + NS].unsqueeze(1).broadcast_to((P, NT, NS)), ALU.is_equal))
                dve.tensor_tensor(hot_tile[:, :, :], hot_tile[:, :, :],
                                  tokm[:, :].unsqueeze(2).broadcast_to((P, NT, NS)), ALU.mult
                                  ).then_inc(r_hi[f], 1)
                for q in range(NQ):
                    dve.tensor_tensor(hot_lane[:, 4 * q:4 * q + 4, :],
                                      lane[:, 4 * q:4 * q + 4].unsqueeze(2).broadcast_to((P, 4, P)),
                                      cst[:, C_PLACE:C_PLACE + P].unsqueeze(1).broadcast_to((P, 4, P)), ALU.is_equal
                                      ).then_inc(r_lo[f], 1)
                chain(dve.tensor_tensor(geq[:, :, :], cst[:, C_T:C_T + NS].unsqueeze(2).broadcast_to((P, NS, NE)),
                                        endt[:, :].unsqueeze(1).broadcast_to((P, NS, NE)), ALU.is_ge))
                chain(dve.tensor_reduce(tef[:, :], geq[:, :, :], AX.X, ALU.add))
                dve.tensor_scalar(te[:, :], tef[:, :], float(NE - 1), None, ALU.min).then_inc(r_te[f], 1)
                dve.wait_ge(r_inv[f], 1)
                chain(dve.tensor_tensor(tokf[:, :], bank[7][:, 0:NS], cst[:, C_SELF:C_END], ALU.add))
                dve.tensor_scalar(tok_g[:, :], tokf[:, :], float(NOTOK), None, ALU.min).then_inc(r_tok[f], 1)
                dve.tensor_copy(tok_s[:, :], tokf[:, :]).then_inc(r_tok[f], 1)

            def expert_tiles(f):
                def relu(t, par, k):
                    dve.wait_ge(e_h[f], t + 1)
                    need(dve, e_y[f], t - 1)
                    for c in range(2, HC):
                        i1 = dve.tensor_scalar(hT[:, par, c, :], bank[3 + 2 * par][:, (c - 2) * P:(c - 1) * P],
                                               ew[:, k, HID + c:HID + c + 1], 0.0,
                                               ALU.add, ALU.max)
                    i1.then_inc(e_hd[f], 1)

                def weights(t, k):
                    e = dve.value_load(te[0:1, bass.ds(t, 1)], min_val=0, max_val=NE - 1)
                    need(dve, e_yc[f], t - 3)
                    dve.tensor_scalar(ew[:, k, :], experts[:, bass.ds(e, 1), 0:WCOLS].rearrange("p a c -> p (a c)"),
                                      1.0, None, ALU.mult).then_inc(e_w[f], 1)

                def out_copy(t, i, k):
                    dve.wait_ge(e_y[f], t + 1)
                    need(dve, e_st[f][k], 16 * i)
                    dve.tensor_tensor(ys_sb[:, k, :], bank[6 + k % 2][:, 0:D], ew[:, k, HID + HC:WCOLS], ALU.add
                                      ).then_inc(e_yc[f], 1)

                def step(t, i, k, do_w=True, do_h=True):
                    if do_h:
                        relu(t + 1, (k + 1) % 2, (k + 1) % 4)
                    out_copy(t, i, k)
                    if do_w:
                        weights(t + 3, (k + 3) % 4)
                dve.wait_ge(r_te[f], 1)
                dve.wait_ge(e_all, 16 * NE)
                weights(0, 0)
                weights(1, 1)
                weights(2, 2)
                relu(0, 0, 0)
                for k in range(4):
                    step(k, 0, k)
                with dve.Fori(1, NS // 4) as i:
                    for k in range(4):
                        step(4 * i + k, i, k)
                for t in range(NS // 4 * 4, NS):
                    step(t, NS // 4, t % 4, do_w=t + 3 < NS, do_h=t + 1 < NS)

            def combine(f, q):
                dve.wait_ge(y_ld[f][q], 16)
                for t in range(4 * q, 4 * q + 4):
                    i1 = dve.scalar_tensor_tensor(x[:, t, :], yg[:, t, :], pr[:, t:t + 1], x[:, t, :],
                                                  ALU.mult, ALU.add)
                i1.then_inc(comb[f], 1)

            layernorm(0)
            dve.wait_ge(gate_s, 32)
            route(0)
            expert_tiles(0)
            layernorm(1)

            def seq(b, bh, k):
                dve.wait_ge(q_v, b + 1)
                dve.tensor_tensor(v[:, bass.ds(2 * b, 2), :],
                                  bank[4 + k][:, 0:2 * D].rearrange("p (t d) -> p t d", t=2),
                                  bv.unsqueeze(1).broadcast_to((P, 2, D)), ALU.add).then_inc(q_vc, 1)
                dve.wait_ge(q_s1, b + 1)
                dve.tensor_tensor(qkr[:, k, :, :], qk[:, k, :, :], spl[:, k, 0, :, :], ALU.subtract
                                  ).then_inc(q_ch, 1)
                dve.wait_ge(q_ch, 2 * b + 1)
                dve.tensor_copy(spl[:, k, 1, :, :], qkr[:, k, :, :]).then_inc(q_ch, 1)
                dve.wait_ge(q_ch, 2 * b + 2)
                dve.tensor_tensor(spl[:, k, 2, :, :], qkr[:, k, :, :], spl[:, k, 1, :, :], ALU.subtract
                                  ).then_inc(q_spl, 1)
            for k in range(2):
                seq(k, 0, k)
            with dve.Fori(1, B // 2) as i:
                for k in range(2):
                    seq(2 * i + k, i, k)

            def max_unit(b, half, u):
                dve.wait_ge(a_s, 12 * b + 6 * half + u + 1)
                pp, w = divmod(u, 3)
                if u == 0:
                    need(dve, a_mb, 2 * b + half - 1)
                if w < 2:
                    dve.tensor_reduce(mh[:, half, 1, 4 * pp + 2 * w:4 * pp + 2 * w + 2],
                                      bank[u % 2][:, :].rearrange("p (h n) -> p h n", h=2), AX.X, ALU.max
                                      ).then_inc(a_mx, 1)
                else:
                    dve.tensor_reduce(mh[:, half, 0, 4 * pp:4 * pp + 4],
                                      bank[u % 2][:, :].rearrange("p (h n) -> p h n", h=4), AX.X, ALU.max
                                      ).then_inc(a_mx, 1)

            def v_spread(b, k):
                need(dve, a_pv, 12 * (b - 1))
                dve.tensor_scalar(va[:, k, :, :, 0:HD], v[:, bass.ds(2 * b, 2), :].rearrange(
                    "p t (h d) -> p t h d", h=NH), 1.0, None, ALU.mult).then_inc(a_va, 1)

            def normalise(b, qt):
                dve.wait_ge(a_oT, 2 * b + qt + 1)
                o = bank[7 - qt][:, :].rearrange("p (g j c) -> p g j c", g=NPAIR, j=2)
                dve.reciprocal(rl[:, qt, :, :], o[:, :, :, HD]).then_inc(a_rl, 1)
                dve.wait_ge(a_rl, 2 * b + qt + 1)
                dve.tensor_tensor(an[:, qt, :].rearrange("p (j g d) -> p g j d", j=2, g=NPAIR), o[:, :, :, 0:HD],
                                  rl[:, qt, :, :].unsqueeze(3).broadcast_to((P, NPAIR, 2, HD)), ALU.mult
                                  ).then_inc(a_an, 1)

            def add_out(b):
                dve.wait_ge(a_wo, b + 1)
                dve.tensor_tensor(x[:, bass.ds(2 * b, 2), :],
                                  bank[7][:, 0:2 * D].rearrange("p (t d) -> p t d", t=2),
                                  x[:, bass.ds(2 * b, 2), :], ALU.add).then_inc(a_x, 1)

            def step(b, k, half, more, first=False):
                for u in range(6):
                    if more:
                        max_unit(b + 1, half, u)
                    if more and half == 0 and u == 2:
                        v_spread(b + 1, 1 - k)
                    if half == 0 and not first:
                        if u == 3:
                            normalise(b - 1, 0)
                        if u == 4:
                            normalise(b - 1, 1)
                    if half == 1 and not first and u == 4:
                        add_out(b - 1)
            dve.wait_ge(q_res, 2 * B)
            dve.wait_ge(q_vc, B)
            dve.wait_ge(static_s, 8)
            v_spread(0, 0)
            for half in range(2):
                for u in range(6):
                    max_unit(0, half, u)
            for half in range(2):
                step(0, 0, half, True, first=True)
            with dve.Fori(0, 3) as i:
                for k in range(2):
                    for half in range(2):
                        step(2 * i + 1 + k, 1 - k, half, True)
            for half in range(2):
                step(7, 1, half, False)
            normalise(7, 0)
            normalise(7, 1)
            add_out(7)
            dve.wait_ge(a_x, B)
            layernorm(2)
            route(1)
            expert_tiles(1)
            for q in range(NQ):
                combine(1, q)

        @block.tensor
        def _(pe):
            pe.wait_ge(cst_s, 16)

            def gate(f):
                def logits(q):
                    pe.wait_ge(g_Tc[f], q + 1)
                    for t in range(4):
                        mm = pe.matmul(bank[2 + q][:, t * NE:(t + 1) * NE], gT[:, q % 2, t * P:(t + 1) * P], wg[:, :],
                                       start=True, stop=True)
                    mm.then_inc(g_lg[f], 1)
                for q in range(NQ):
                    pe.wait_ge(ln_xn[2 * f], q + 1)
                    if q >= 2:
                        pe.wait_ge(g_Tc[f], q - 1)
                    for t in range(4):
                        mm = pe.transpose(bank[q % 2][:, t * P:(t + 1) * P], xn[:, 4 * q + t, :], ident)
                    mm.then_inc(g_T[f], 1)
                    if q == 1 and f == 0:
                        pe.wait_ge(gate_s, 32)
                    if q >= 1:
                        logits(q - 1)
                logits(NQ - 1)
                pe.wait_ge(r_oh[f], 1)
                oh_ = onehot[:, :, :].rearrange("p t e -> p (t e)")
                pe.matmul(bank[6][:, 0:P], cb[:, C_UP:C_UP + P], oh_, start=True, stop=True)
                pe.matmul(bank[6][:, P:2 * P], cb[:, C_ONE:C_ONE + P], oh_, start=True, stop=True
                          ).then_inc(r_cnt[f], 1)
                pe.wait_ge(r_hi[f], 1)
                for t in range(NT):
                    if t % 4 == 0:
                        pe.wait_ge(r_lo[f], t // 4 + 1)
                    mm = pe.matmul(bank[7][:, 0:NS], hot_lane[:, t, :], hot_tile[:, t, :],
                                   start=(t == 0), stop=(t == NT - 1))
                mm.then_inc(r_inv[f], 1)

            def expert_tiles(f):
                def turn(t, i, k):
                    pe.wait_ge(e_xs[f][k], 16 * (i + 1))
                    need(pe, e_Tc[f], t - 1)
                    pe.transpose(bank[k % 2][:, 0:P], xs_sb[:, k, :], ident).then_inc(e_T[f], 1)

                def hidden(t, i, k):
                    pe.wait_ge(e_Tc[f], t + 1)
                    pe.wait_ge(e_w[f], t + 1)
                    need(pe, e_ha[f], t - 1)
                    need(pe, e_hd[f], t - 1)
                    for c in range(HC):
                        mm = pe.matmul(bank[2 + 2 * (k % 2) + c // 2][:, (c % 2) * P:(c % 2 + 1) * P],
                                       ew[:, k, c * P:(c + 1) * P], xsT[:, k % 2, :], start=True, stop=True)
                    mm.then_inc(e_h[f], 1)

                def output(t, k):
                    e = pe.value_load(te[0:1, bass.ds(t, 1)], min_val=0, max_val=NE - 1)
                    pe.wait_ge(e_ha[f], t + 1)
                    pe.wait_ge(e_hd[f], t + 1)
                    need(pe, e_yc[f], t - 1)
                    for c in range(HC):
                        mm = pe.matmul(bank[6 + k % 2][:, 0:D], hT[:, k % 2, c, :],
                                       experts[:, bass.ds(e, 1), WCOLS + c * D:WCOLS + (c + 1) * D].rearrange("p a c -> p (a c)"), start=(c == 0), stop=(c == HC - 1))
                    mm.then_inc(e_y[f], 1)

                def step(t, i, k, do_T=True, do_h=True):
                    if do_T:
                        turn(t + 2, i + (k + 2) // 4, (k + 2) % 4)
                    if do_h:
                        hidden(t + 1, i + (k + 1) // 4, (k + 1) % 4)
                    output(t, k)
                turn(0, 0, 0)
                turn(1, 0, 1)
                hidden(0, 0, 0)
                for k in range(4):
                    step(k, 0, k)
                with pe.Fori(1, NS // 4) as i:
                    for k in range(4):
                        step(4 * i + k, i, k)
                for t in range(NS // 4 * 4, NS):
                    step(t, NS // 4, t % 4, do_T=t + 2 < NS, do_h=t + 1 < NS)

            pe.wait_ge(cb_s, 1)
            gate(0)
            expert_tiles(0)

            pe.wait_ge(attw_s, 32)

            def seq(b, k):
                pe.wait_ge(q_xb, b + 1)
                need(pe, q_Tc, b - 1)
                for t in range(2):
                    mm = pe.transpose(bank[k][:, t * P:(t + 1) * P], xb[:, k, t, :], ident)
                mm.then_inc(q_T, 1)
                pe.wait_ge(q_Tc, b + 1)
                need(pe, q_qkc, b - 1)
                for t in range(2):
                    mm = pe.matmul(bank[2 + k][:, t * T:(t + 1) * T], wt[:, t, :], xbT[:, k, :],
                                   start=True, stop=True)
                mm.then_inc(q_qk, 1)
                need(pe, q_vc, b - 1)
                for t in range(2):
                    mm = pe.matmul(bank[4 + k][:, t * D:(t + 1) * D], xbT[:, k, t * P:(t + 1) * P], wt[:, 2, :],
                                   start=True, stop=True)
                mm.then_inc(q_v, 1)
            for k in range(2):
                seq(k, k)
            with pe.Fori(1, B // 2) as i:
                for k in range(2):
                    seq(2 * i + k, k)
            pe.wait_ge(q_qkc, B)
            pe.wait_ge(q_vc, B)

            maskS = cb[:, C_MS:C_MS + P]
            maskT = cb[:, C_MT:C_MT + P]

            def scores_q(b, bh, k, half, u):
                pp, w = divmod(u, 3)
                if u == 0:
                    pe.wait_ge(a_stk[k][half], 64 * (bh + 1))
                need(pe, a_mx, 12 * b + 6 * half + u - 1)
                o = bank[u % 2]
                if w < 2:
                    pair = 4 * half + 2 * pp + w
                    ov = o[:, :].rearrange("p (j n) -> p j n", j=2)
                    pe.matmul(ov[:, :, P:T], ident_b, maskS.unsqueeze(1).broadcast_to((P, 2, P)),
                              start=True, stop=False, **MM_BANK)
                    for j in range(2):
                        mm = pe.matmul(ov[:, j, :], qz[k][0:SROWS, pair, j, P:T], ks[k][0:SROWS, pair, :],
                                       start=False, stop=True, **MM_BANK)
                else:
                    ov = o[:, :].rearrange("p (h n) -> p h n", h=4)
                    pe.matmul(ov, ident_b, maskS.unsqueeze(1).broadcast_to((P, 4, P)),
                              start=True, stop=False, **MM_BANK)
                    for h in range(4):
                        pair = 4 * half + 2 * pp + h // 2
                        mm = pe.matmul(ov[:, h, :], qz[k][0:SROWS, pair, h % 2, 0:P], ks[k][0:SROWS, pair, 0:P],
                                       start=False, stop=True, **MM_BANK)
                mm.then_inc(a_s, 1)

            def scores_k(b, k, half, u):
                pp, w = divmod(u, 3)
                if u == 0:
                    pe.wait_ge(a_m[half], 16 * (b + 1))
                need(pe, a_e, 12 * b + 6 * half + u - 1)
                o = bank[2 + u % 2]
                if w < 2:
                    pair = 4 * half + 2 * pp + w
                    ov = o[:, :].rearrange("p (j n) -> p j n", j=2)
                    pe.matmul(ov[:, :, 0:P], ident_b, maskT.unsqueeze(1).broadcast_to((P, 2, P)),
                              start=True, stop=False, **MM_BANK)
                    mm = pe.matmul(ov, ks[k][0:KROWS, pair, 0:P], qz[k][0:KROWS, pair, :, :],
                                   start=False, stop=True, **MM_BANK)
                else:
                    ov = o[:, :].rearrange("p (i j n) -> p i j n", i=2, j=2)
                    pe.matmul(o[:, :].rearrange("p (h n) -> p h n", h=4), ident_b,
                              maskT.unsqueeze(1).broadcast_to((P, 4, P)), start=True, stop=False, **MM_BANK)
                    for i in range(2):
                        pair = 4 * half + 2 * pp + i
                        mm = pe.matmul(ov[:, i, :, :], ks[k][0:KROWS, pair, P:T], qz[k][0:KROWS, pair, :, P:T],
                                       start=False, stop=True, **MM_BANK)
                mm.then_inc(a_st, 1)

            def pv(b, k, half, u):
                pp, w = divmod(u, 3)
                n = 12 * b + 6 * half + u
                pe.wait_ge(a_e, n + 1)
                if u == 0:
                    need(pe, a_ot, 2 * b + half - 1)
                    if half == 0:
                        pe.wait_ge(a_va, b + 1)
                o = bank[4 + half]
                p_ = pT[:, (6 * half + u) % 4, :]
                for h in range(4) if w == 2 else range(2 * w, 2 * w + 2):
                    pair, j = 4 * half + 2 * pp + h // 2, h % 2
                    if w < 2:
                        mm = pe.matmul(o[32 * h:32 * h + 32, pp * T:(pp + 1) * T], va[:, k, 0, 8 * j + pair, :],
                                       p_[:, j * T:(j + 1) * T], start=True, stop=False, **MM_BANK)
                    else:
                        mm = pe.matmul(o[32 * h:32 * h + 32, pp * T + P:(pp + 1) * T], va[:, k, 1, 8 * j + pair, :],
                                       p_[:, h * P:(h + 1) * P], start=False, stop=True, **MM_BANK)
                mm.then_inc(a_pv, 1)

            def turn_max(b, half):
                pe.wait_ge(a_mb, 2 * b + half + 1)
                o = bank[6][0:24, 0:P].bitcast(BF16)
                for qt in range(2):
                    mm = pe.transpose(o[:, qt * P:(qt + 1) * P],
                                      mb[:, half, qt, :, :].rearrange("p s h -> p (s h)"), ident_b)
                mm.then_inc(a_mt, 1)

            def turn_out(b, qt):
                pe.wait_ge(a_ot, 2 * b + 2)
                for g in range(4):
                    mm = pe.transpose(bank[7 - qt][:, g * P:(g + 1) * P], oT[g // 2][:, g % 2, qt * P:(qt + 1) * P],
                                      ident)
                mm.then_inc(a_oT, 1)

            def turn_norm(b):
                pe.wait_ge(a_an, 2 * b + 2)
                for qt in range(2):
                    mm = pe.transpose(bank[7][:, qt * P:(qt + 1) * P], an[:, qt, :], ident)
                mm.then_inc(a_aT, 1)

            def project(b):
                pe.wait_ge(a_aTc, b + 1)
                for qt in range(2):
                    mm = pe.matmul(bank[7][:, qt * D:(qt + 1) * D], anT[:, qt * P:(qt + 1) * P], wt[:, 3, :],
                                   start=True, stop=True)
                mm.then_inc(a_wo, 1)

            def step(b, bh, k, half, more, first=False):
                for u in range(6):
                    scores_k(b, k, half, u)
                    if more:
                        scores_q(b + 1, bh, 1 - k, half, u)
                    if u > 0:
                        pv(b, k, half, u - 1)
                    elif half:
                        pv(b, k, 0, 5)
                    elif not first:
                        pv(b - 1, 1 - k, 1, 5)
                    if u == 1:
                        if half == 0:
                            if not first:
                                pe.wait_ge(a_mtc, 2 * b + 1)
                            turn_max(b, 1)
                        elif more:
                            if not first:
                                pe.wait_ge(a_an, 2 * b)
                            pe.wait_ge(a_mtc, 2 * b + 2)
                            turn_max(b + 1, 0)
                    if half == 0 and not first:
                        if u == 2:
                            need(pe, a_x, b - 1)
                            turn_out(b - 1, 0)
                        if u == 3:
                            pe.wait_ge(a_mtc, 2 * b + 2)
                            turn_out(b - 1, 1)
                        if u == 5:
                            turn_norm(b - 1)
                    if half == 1 and not first and u == 3:
                        project(b - 1)
            for half in range(2):
                for u in range(6):
                    scores_q(0, 0, 0, half, u)
            turn_max(0, 0)
            pe.wait_ge(a_mtc, 1)
            for half in range(2):
                step(0, 0, 0, half, True, first=True)
            with pe.Fori(0, 3) as i:
                for half in range(2):
                    step(2 * i + 1, i + 1, 1, half, True)
                for half in range(2):
                    step(2 * i + 2, i + 1, 0, half, True)
            for half in range(2):
                step(7, 3, 1, half, False)
            pv(7, 1, 1, 5)
            pe.wait_ge(a_x, 7)
            turn_out(7, 0)
            turn_out(7, 1)
            turn_norm(7)
            project(7)
            gate(1)
            expert_tiles(1)


_INS = ["x", "wqkvo", "bqk", "rows", "w_gate", "experts", "const"]


def kernel(L0_attn_x, L0_attn_norm_w, L0_attn_Wq, L0_attn_bq, L0_attn_Wk, L0_attn_bk, L0_attn_Wv, L0_attn_bv,
           L0_attn_Wo, L0_attn_bo, L0_ffn_w_gate, L0_ffn_b_gate, L0_ffn_W1, L0_ffn_b1, L0_ffn_W2, L0_ffn_b2):
    import concourse.bacc as bacc
    from concourse.bass_utils import run_bass_kernel_spmd

    f = lambda a: np.asarray(a)
    perm = np.arange(D).reshape(2, NPAIR, HD).transpose(0, 2, 1).reshape(-1)
    wq, wk, wv, wo = (f(w).T for w in (L0_attn_Wq, L0_attn_Wk, L0_attn_Wv, L0_attn_Wo))
    pad = np.zeros(D - NE, f(L0_ffn_b_gate).dtype)
    w2 = f(L0_ffn_W2).reshape(NE, HC, P, D).transpose(0, 2, 1, 3).reshape(NE, P, HC * D)
    b2 = np.broadcast_to(f(L0_ffn_b2)[:, None, :], (NE, P, D))
    b1 = f(L0_ffn_b1).reshape(NE, HC, P).transpose(0, 2, 1)
    arrays = {
        "x": f(L0_attn_x).reshape(B * T, D),
        "wqkvo": np.stack([wq[:, perm], wk[:, perm], wv, wo], axis=1),
        "bqk": np.stack([f(L0_attn_bq)[perm], f(L0_attn_bk)[perm]], axis=1),
        "rows": np.concatenate([f(L0_attn_norm_w), f(L0_attn_bv), f(L0_attn_bo), f(L0_ffn_b_gate), pad]),
        "w_gate": f(L0_ffn_w_gate),
        "experts": np.concatenate([f(L0_ffn_W1), b1, b2, w2], axis=2).reshape(NE * P, ECOLS),
        "const": constants(),
    }
    nc = bacc.Bacc("TRN2", target_bir_lowering=False, num_devices=1)
    arrays = {f"in_{n}": np.ascontiguousarray(arrays[n]) for n in _INS}
    args = [nc.dram_tensor(n, a.shape, mybir.dt.from_np(a.dtype), kind="ExternalInput").ap()
            for n, a in arrays.items()]
    out = nc.dram_tensor("out_0", (B * T, D), F32, kind="ExternalOutput").ap()
    build(nc, *args, out)
    r = run_bass_kernel_spmd(nc, [arrays], core_ids=[0])
    return r.results[0]["out_0"].reshape(B, T, D)
```

```python
from contextlib import ExitStack

import numpy as np
import concourse.bass as bass
from concourse import mybir

F32 = mybir.dt.float32
BF16 = mybir.dt.bfloat16
I32 = mybir.dt.int32
U32 = mybir.dt.uint32
ALU = mybir.AluOpType
ACT = mybir.ActivationFunctionType
AX = mybir.AxisListType

P = 128
D = 128
B, T = 8, 256
NT = B * T // P
NQ = NT // 4
NE, HID = 8, 512
HC = HID // P
NS = NT + NE - 1
WCOLS = HID + HC + D
ECOLS = WCOLS + HC * D
SPL = 3
RING = 6
OUT = 3
WRING = 3
AHEAD = RING + 0
NOTOK = NT * P
NH, HD = 16, 8
NPAIR = NH // 2
BLK = 6
JROWS = BLK * HD
SROWS = 2 * JROWS
MROW = SROWS
KROWS = MROW + 3
LN_EPS, RMS_EPS = 1e-5, 1e-6
NEG = -1e30
SCALE = 1.0 / float(np.sqrt(np.float32(HD)))

C_ID, C_UP, C_MS, C_ONE, C_J, C_REV, C_T = 0, 128, 256, 384, 512, 528, 536
C_MHALF = C_T + NS
C_PLACE = C_MHALF + 4
C_TOK = C_PLACE + P
C_LANE = C_TOK + NT
C_SELF = C_LANE + 1
C_END = C_SELF + NS


def constants():
    c = np.zeros((P, C_END), np.float32)
    i = np.arange(P)
    c[:, C_ID:C_ID + P] = np.eye(P)
    c[:, C_UP:C_UP + P] = i[:, None] < i[None, :]
    c[:, C_MS:C_MS + P] = np.where(i[None, :] > i[:, None], NEG, 0)
    c[:, C_ONE:C_ONE + P] = 1
    c[:, C_J:C_J + NT] = P * np.arange(NT)
    c[:, C_REV:C_REV + NE] = NE - np.arange(NE)
    c[:, C_T:C_T + NS] = np.arange(NS)
    c[:, C_MHALF:C_MHALF + 4] = -0.5
    c[:, C_PLACE:C_PLACE + P] = i
    c[:, C_TOK:C_TOK + NT] = P * np.arange(NT) - NOTOK
    c[:, C_LANE] = i
    c[:, C_SELF:C_END] = NOTOK + P * np.arange(NS) + i[:, None]
    return c


def build(nc, x_in, wqkvo, cols_in, rows_in, w_gate, experts_in, const_in, out):
    ctx = ExitStack()
    with ctx:
        def sb(name, shape, dt=F32):
            return ctx.enter_context(nc.sbuf_tensor(name, shape, dt))

        def sem(name):
            return ctx.enter_context(nc.semaphore(name))

        def sems(name, n):
            return [sem(f"{name}{i}") for i in range(n)]

        bank = [ctx.enter_context(nc.psum_tensor(f"bank{i}", [P, 512], F32)) for i in range(8)]

        x = sb("x", [P, NT, D])
        xn = sb("xn", [P, NT, D])
        cst = sb("cst", [P, C_END])
        cb = sb("cb", [P, C_J], BF16)
        wt = sb("wt", [P, 4, D])
        cols = sb("cols", [P, 3])
        rows = sb("rows", [P, 4 * D])
        experts = sb("experts", [P, NE, ECOLS])
        wg = sb("wg", [D, NE])
        ident = cst[:, C_ID:C_ID + P]
        ident_b = cb[:, C_ID:C_ID + P]
        norm_w, bv, bo = (rows[:, i * D:(i + 1) * D] for i in range(3))
        b_gate = rows[:, 3 * D:3 * D + NE]

        st6 = sb("st6", [P, NT, 6])
        mv = sb("mv", [P, NT, 2])
        vs = sb("vs", [P, NT])
        nb = sb("nb", [P, NT])
        rs = sb("rs", [P, NT])

        gT = sb("gT", [P, 2, 512])
        lg = sb("lg", [P, NT, NE])
        sh = sb("sh", [P, NT, NE])
        ex = sb("ex", [P, NT, NE])
        mx = sb("mx", [P, NT])
        den = sb("den", [P, NT])
        pr = sb("pr", [P, NT])
        oh = sb("oh", [P, NT, NE])
        pick = sb("pick", [P, NT, NE])
        best = sb("best", [P, NT])
        onehot = sb("onehot", [P, NT, NE], BF16)
        tot = sb("tot", [P, NE, NT])
        upto = sb("upto", [P, NE, NT])
        rank = sb("rank", [P, NT, NE])
        keep = sb("keep", [P, NE, NT])
        base = sb("base", [P, NE, NT])
        gtj = sb("gtj", [P, NE, NT])
        ntl = sb("ntl", [P, NE])
        endt = sb("endt", [P, NE])
        begt = sb("begt", [P, NE])
        ones8 = sb("ones8", [P, NE])
        slotm = sb("slotm", [P, NT, NE])
        slotf = sb("slotf", [P, NT])
        sloti = sb("sloti", [P, NT], I32)
        tilei = sb("tilei", [P, NT], I32)
        tilef = sb("tilef", [P, NT])
        lane = sb("lane", [P, NT])
        dlane = sb("dlane", [P, NT])
        dtile = sb("dtile", [P, NT])
        hot = sb("hot", [P, NT, NS])
        hot_tile = sb("hot_tile", [P, NT, 2, NS], BF16)
        hot_lane = sb("hot_lane", [P, NT, P], BF16)
        tokf = sb("tokf", [P, NS])
        tok_s = sb("tok_s", [P, NS], U32)
        tok_g = sb("tok_g", [P, NS], U32)
        geq = sb("geq", [P, NS, NE])
        tef = sb("tef", [P, NS])
        te = sb("te", [P, NS], I32)

        zero = sb("zero", [P, D])
        xs_sb = sb("xs_sb", [P, RING, D])
        ew = sb("ew", [P, WRING, WCOLS])
        xsT = sb("xsT", [P, 2, P])
        hT = sb("hT", [P, 2, HC, P])
        ys_sb = sb("ys_sb", [P, OUT, D])
        yg = sb("yg", [P, NT, D])

        res = sb("res", [P, 4, D])
        xnT = sb("xnT", [P, 2, 4 * P])
        qkr = sb("qkr", [P, 2, 2, 4 * P])
        spl = sb("spl", [P, SPL, 4, 2, 4 * P], BF16)
        v = sb("v", [P, NT, D])
        va = sb("va", [P, 2, 2, NH, 32])
        qz = [sb(f"qz{i}", [P, 2, 2, 4, T], BF16) for i in range(2)]
        ks = [sb(f"ks{i}", [P, NPAIR, T], BF16) for i in range(2)]
        mh = sb("mh", [P, 2, 2, 2, 4])
        mr = sb("mr", [P, 2, 2, 8])
        mb = sb("mb", [P, 2, 2, 3, 8], BF16)
        turn = sb("turn", [P, 4])
        mT = sb("mT", [24, 2, T], BF16)
        pT = sb("pT", [P, 6, 512])
        oT = [sb(f"oT{i}", [P, 2, T]) for i in range(2)]
        rl = sb("rl", [P, 2, NPAIR, 2])
        an = sb("an", [P, 2, D])
        anT = sb("anT", [P, T])

        xn_d = nc.dram_tensor("xn_d", [NOTOK + 1, D], F32, kind="Internal").ap()
        y_d = nc.dram_tensor("y_d", [NOTOK + NS * P, D], F32, kind="Internal").ap()
        sp_d = nc.dram_tensor("sp_d", [B * 2 * BLK * P, T], BF16, kind="Internal").ap()

        x_in_s = sems("x_loaded", NQ)
        cst_s = sem("const_loaded")
        gate_s = sem("gate_loaded")
        attw_s = sem("attn_weights_loaded")
        zero_s = sem("zero_set")
        cb_s = sem("const_bf16")
        notok_s = sem("no_token_row_zeroed")
        static_s = sem("static_buffers_set")
        final_s = sem("out_written")
        ln_st = sems("ln_stats", 3)
        ln_mv = sems("ln_meanvar", 3)
        ln_vs = sems("ln_shifted_var", 3)
        ln_rs = sems("ln_scale", 3)
        ln_nb = sems("ln_bias", 3)
        ln_xa = sems("ln_normalised_act", 3)
        ln_xn = sems("ln_normalised", 3)
        g_T = sems("gate_transposed", 2)
        g_Tc = sems("gate_transpose_copied", 2)
        g_lg = sems("gate_logits", 2)
        r_ch = sems("route_chain", 2)
        r_sh = sems("route_shifted", 2)
        r_ex = sems("route_exp", 2)
        r_oh = sems("route_onehot", 2)
        r_cnt = sems("route_counts", 2)
        r_te = sems("route_tile_experts", 2)
        r_rank = sems("route_rank", 2)
        r_hot = sems("route_tile_equal", 2)
        r_hi = sems("route_hot_tile", 2)
        r_lo = sems("route_hot_lane", 2)
        r_inv = sems("route_inverse", 2)
        r_tok = sems("route_tokens", 2)
        xn_st = sems("xn_stored", 2)
        e_all = sem("experts_loaded")
        e_w = sems("expert_weights_copied", 2)
        e_xs = [sems(f"tile_gathered{f}_", RING) for f in range(2)]
        e_T = sems("sorted_transposed", 2)
        e_Tc = sems("sorted_transpose_copied", 2)
        e_h = sems("hidden_product", 2)
        e_ha = sems("hidden_relu_act", 2)
        e_hd = sems("hidden_relu_dve", 2)
        e_y = sems("out_product", 2)
        e_yc = sems("out_copied", 2)
        e_st = [sems(f"out_scattered{f}_", OUT) for f in range(2)]
        y_ld = [sems(f"y_loaded{f}_", NQ) for f in range(2)]
        comb = sems("combined", 2)

        w_nw = sem("weights_scaled")
        q_res = sem("residual_chain")
        q_T = sem("quad_transposed")
        q_Tc = sem("quad_transpose_copied")
        q_qk = sem("quad_qk_product")
        q_v = sem("quad_v_product")
        q_vc = sem("quad_v_copied")
        q_s1 = sem("quad_split1")
        q_r = sem("quad_split1_rest")
        q_s2 = sem("quad_split2")
        q_spl = sem("quad_split3")
        q_std = sems("quad_splits_stored", NQ)
        a_va = sem("attn_v_spread")
        a_stk = [sems(f"stack_loaded{i}_", 2) for i in range(2)]
        a_s = sem("scores_q")
        a_mx = sem("scores_max")
        a_mch = sem("max_split_chain")
        a_mb = sem("max_split")
        a_mt = sem("max_transposed")
        a_mtc = sem("max_transpose_copied")
        a_m = sems("max_rows_loaded", 2)
        a_st = sem("scores_k")
        a_e = sem("exp_done")
        a_pm = sem("exp_masked")
        a_pv = sem("pv_done")
        a_ot = sem("attn_out_copied")
        a_oT = sem("attn_out_transposed")
        a_rl = sem("attn_recip")
        a_an = sem("attn_normalised")
        a_aT = sem("attn_norm_transposed")
        a_aTc = sem("attn_norm_transpose_copied")
        a_wo = sem("attn_projected")
        a_x = sem("attn_added")

        def need(eng, s, n):
            if not isinstance(n, int) or n > 0:
                eng.wait_ge(s, n)

        def shared(n, q):
            return n < 2 or q == NQ - 1

        MM_BANK = dict(skip_group_check=True)
        block = ctx.enter_context(nc.Block())
        t_rows = BLK * P

        @block.sync
        def _(sp):
            xv = x_in.rearrange("(t p) d -> p t d", p=P)
            for q in range(NQ):
                sp.dma_start(x[:, 4 * q:4 * q + 4, :], xv[:, 4 * q:4 * q + 4, :]).then_inc(x_in_s[q], 16)
                if q == 0:
                    sp.dma_start(cst[:, :], const_in).then_inc(cst_s, 16)
            sp.dma_start(wg[:, :], w_gate).then_inc(gate_s, 16)
            sp.dma_start(rows[:, :], rows_in.partition_broadcast(P)).then_inc(gate_s, 16)
            sp.dma_start(wt[:, :, :], wqkvo).then_inc(attw_s, 16)
            sp.dma_start(cols[:, :], cols_in).then_inc(attw_s, 16)
            for e in range(NE):
                sp.dma_start(experts[:, e, :], experts_in[e * P:(e + 1) * P, :]).then_inc(e_all, 16)
            sp.wait_ge(zero_s, 1)
            sp.dma_start(xn_d[NOTOK:NOTOK + 1, :], zero[0:1, :]).then_inc(notok_s, 16)

            def tok_view(dram, q):
                return dram[4 * q * P:4 * (q + 1) * P, :].rearrange("(t p) d -> p t d", p=P)

            def xn_stores(f):
                for q in range(NQ):
                    sp.wait_ge(ln_xn[2 * f], q + 1)
                    if shared(2 * f, q):
                        sp.wait_ge(ln_xa[2 * f], q + 1 if f == 0 else 1)
                    sp.dma_start(tok_view(xn_d, q), xn[:, 4 * q:4 * q + 4, :]).then_inc(xn_st[f], 16)

            def y_loads(f):
                for k in range(OUT):
                    sp.wait_ge(e_st[f][k], 16 * ((NS - k + OUT - 1) // OUT))
                for q in range(NQ):
                    sp.dma_start(yg[:, 4 * q:4 * q + 4, :], tok_view(y_d, q)).then_inc(y_ld[f][q], 16)

            def split_stores(*seqs):
                for b in seqs:
                    q = b // 2
                    sp.wait_ge(q_spl, q + 1)
                    toks = slice(b % 2 * T, (b % 2 + 1) * T)
                    for t, first, last in ((0, spl[:, q % SPL, 0:1, 0, toks].broadcast_to((P, 3, T)),
                                            spl[:, q % SPL, 1:4, 0, toks]),
                                           (1, spl[:, q % SPL, 1:4, 1, toks], spl[:, q % SPL, 0:3, 1, toks])):
                        dst = sp_d[(2 * b + t) * t_rows:(2 * b + t + 1) * t_rows, :].rearrange(
                            "(c r) n -> r c n", c=BLK)
                        sp.dma_start(dst[:, 0:3, :], first).then_inc(q_std[q], 16)
                        sp.dma_start(dst[:, 3:6, :], last).then_inc(q_std[q], 16)

            def stack_load(b, k, half):
                r0 = b * (2 * t_rows) if isinstance(b, int) else sp.snap(b * (2 * t_rows))
                need(sp, a_st, 12 * (b - 2) + 6 * half + 6)
                for j in range(2):
                    rows_j = slice(JROWS * j, JROWS * (j + 1))
                    for t, buf in ((0, qz[k][rows_j, half, j, :, :]),
                                   (1, ks[k][rows_j, 4 * half:4 * half + 4, :])):
                        src = sp_d[bass.ds(r0 + t * t_rows, t_rows), :].rearrange("(c g r) n -> c g (r n)", c=BLK, g=4)
                        sp.dma_start(buf, src[:, 2 * half + j, :]).then_inc(a_stk[k][half], 16)

            def max_rows(b, k, half):
                sp.wait_ge(a_mtc, 2 * b + half + 1)
                sp.dma_start(qz[k][MROW:MROW + 3, half, :, :, :].rearrange("s j i n -> s (j i n)"), mT[:, half, :]
                             ).then_inc(a_m[half], 16)

            xn_stores(0)
            y_loads(0)
            sp.wait_ge(static_s, 6)
            split_stores(0, 1)
            sp.wait_ge(q_std[0], 128)
            for half in range(2):
                stack_load(0, 0, half)
            split_stores(2, 3)
            for half in range(2):
                stack_load(1, 1, half)

            def step(b, k, half, more, stores=()):
                if half == 0:
                    max_rows(b, k, 1)
                elif more >= 1:
                    max_rows(b + 1, 1 - k, 0)
                split_stores(*stores)
                if more >= 2:
                    stack_load(b + 2, k, half)
            max_rows(0, 0, 0)
            split_stores(4, 5)
            sp.wait_ge(q_std[1], 128)
            for half in range(2):
                step(0, 0, half, 2, stores=(6 + half,))
            for q in range(2, NQ):
                sp.wait_ge(q_std[q], 128)
            with sp.Fori(0, 2) as i:
                for half in range(2):
                    step(2 * i + 1, 1, half, 2)
                for half in range(2):
                    step(2 * i + 2, 0, half, 2)
            for b, more in ((5, 2), (6, 1), (7, 0)):
                for half in range(2):
                    step(b, b % 2, half, more)
            xn_stores(1)
            y_loads(1)
            ov = out.rearrange("(t p) d -> p t d", p=P)
            for q in range(NQ):
                sp.wait_ge(comb[1], q + 1)
                sp.dma_start(ov[:, 4 * q:4 * q + 4, :], x[:, 4 * q:4 * q + 4, :]).then_inc(final_s, 16)
            sp.wait_ge(final_s, 16 * NQ)

        @block.gpsimd
        def _(pool):
            pool.memset(zero[:, :], 0.0).then_inc(zero_s, 1)

            def ln_scale(n, q):
                tiles = slice(4 * q, 4 * q + 4)
                mul, add = (1.0 + RMS_EPS, RMS_EPS * LN_EPS) if n == 1 else (1.0, LN_EPS)
                pool.wait_ge(ln_mv[n], q + 1)
                pool.tensor_scalar(vs[:, tiles], mv[:, tiles, 1], mul, add, ALU.mult, ALU.add
                                   ).then_inc(ln_vs[n], 1)
                pool.wait_ge(ln_vs[n], q + 1)
                pool.tensor_tensor(rs[:, tiles], vs[:, tiles], cst[:, C_MHALF:C_MHALF + 4], ALU.pow
                                   ).then_inc(ln_rs[n], 1)

            def hot_tiles(f):
                pool.wait_ge(r_hot[f], 1)
                for part, d in enumerate((dlane, dtile)):
                    i1 = pool.tensor_tensor(hot_tile[:, :, part, :], hot[:, :, :],
                                            d[:, :].unsqueeze(2).broadcast_to((P, NT, NS)), ALU.mult)
                i1.then_inc(r_hi[f], 1)

            def expert_tiles(f):
                def gather(t):
                    need(pool, e_T[f], t - RING + 1)
                    pool.indirect_dma_start(xs_sb[:, t % RING, :], None, xn_d[:, :],
                                            bass.IndirectOffsetOnAxis(ap=tok_g[:, t:t + 1], axis=0)
                                            ).then_inc(e_xs[f][t % RING], 16)

                def scatter(t):
                    pool.wait_ge(e_yc[f], t + 1)
                    pool.indirect_dma_start(y_d[:, :], bass.IndirectOffsetOnAxis(ap=tok_s[:, t:t + 1], axis=0),
                                            ys_sb[:, t % OUT, :], None).then_inc(e_st[f][t % OUT], 16)

                pool.wait_ge(xn_st[f], 16 * NQ)
                if f == 0:
                    pool.wait_ge(notok_s, 16)
                pool.wait_ge(r_tok[f], 2)
                for t in range(AHEAD):
                    gather(t)
                for t in range(NS):
                    if t + AHEAD < NS:
                        gather(t + AHEAD)
                    scatter(t)

            pool.wait_ge(cst_s, 16)
            for q in range(NQ):
                ln_scale(0, q)
            for k in range(2):
                pool.memset(qz[k][:, :, :, :, :].rearrange("p h j i n -> p (h j i n)").bitcast(F32), 0.0
                            ).then_inc(static_s, 1)
                pool.memset(ks[k][:, :, :], -1.0).then_inc(static_s, 1)
            pool.memset(va[:, :, :, :, :], 0.0).then_inc(static_s, 1)
            pool.wait_ge(static_s, 5)
            pool.memset(va[:, :, :, :, HD:HD + 1], 1.0).then_inc(static_s, 1)
            hot_tiles(0)
            expert_tiles(0)

            def residual(q):
                tiles = slice(4 * q, 4 * q + 4)
                bc = lambda row: row.unsqueeze(1).broadcast_to((P, 4, D))
                pool.wait_ge(ln_xn[1], q + 1)
                pool.wait_ge(ln_xa[1], q + 1)
                if q > 0:
                    pool.wait_ge(q_res, 3 * q)
                pool.tensor_tensor(res[:, :, :], xn[:, tiles, :], bc(norm_w), ALU.mult).then_inc(q_res, 1)
                pool.wait_ge(q_res, 3 * q + 1)
                pool.tensor_tensor(res[:, :, :], res[:, :, :], bc(bo), ALU.add).then_inc(q_res, 1)
                pool.wait_ge(q_res, 3 * q + 2)
                pool.tensor_tensor(x[:, tiles, :], x[:, tiles, :], res[:, :, :], ALU.add).then_inc(q_res, 1)
            ln_scale(1, 0)
            for q in range(1, NQ):
                ln_scale(1, q)
                residual(q - 1)
            residual(NQ - 1)

            def max_split(b, half):
                n = 2 * b + half
                pool.wait_ge(a_mx, 6 * n + 6)
                need(pool, a_mt, n - 1)
                z_ = zero[:, 0:16].rearrange("p (q h) -> p q h", q=2)
                m_ = mh[:, half, :, :, :].rearrange("p q j h -> p q (j h)")
                r_, s_ = mr[:, half, :, :], mb[:, half, :, :, :]
                pool.tensor_tensor(s_[:, :, 0, :], m_, z_, ALU.add).then_inc(a_mch, 1)
                pool.wait_ge(a_mch, 4 * n + 1)
                pool.tensor_tensor(r_, m_, s_[:, :, 0, :], ALU.subtract).then_inc(a_mch, 1)
                pool.wait_ge(a_mch, 4 * n + 2)
                pool.tensor_tensor(s_[:, :, 1, :], r_, z_, ALU.add).then_inc(a_mch, 1)
                pool.wait_ge(a_mch, 4 * n + 3)
                pool.tensor_tensor(r_, r_, s_[:, :, 1, :], ALU.subtract).then_inc(a_mch, 1)
                pool.wait_ge(a_mch, 4 * n + 4)
                pool.tensor_tensor(s_[:, :, 2, :], r_, z_, ALU.add).then_inc(a_mb, 1)

            def mask(b, half, pp, late):
                pool.wait_ge(a_e, 12 * b + 6 * half + 3 * pp + 2 + late)
                n = 2 * pp + late
                need(pool, a_pm, 8 * b + 4 * half + n - 3)
                pool.tensor_tensor(turn[:, n:n + 1], zero[:, 0:1], zero[:, 0:1], ALU.add)
                if late:
                    p_ = pT[:, 3 * pp + 2, :].rearrange("p (h n) -> p h n", h=4)
                else:
                    p_ = pT[:, 3 * pp:3 * pp + 2, :].rearrange("p u (j n) -> p (u j) n", j=2)[:, :, 0:P]
                pool.affine_select(out=p_, in_=p_, pattern=[[0, 4], [1, P]], compare_op=ALU.is_ge, fill=0.0,
                                   base=0, channel_multiplier=-1).then_inc(a_pm, 1)

            def step(b, half, more=True):
                if half == 0:
                    max_split(b, 1)
                elif more:
                    max_split(b + 1, 0)
                for n in range(4):
                    mask(b, half, n // 2, n % 2)
                    if not more and (half, n) in SCALE_AT:
                        ln_scale(2, SCALE_AT[half, n])
            SCALE_AT = {(0, 3): 0, (1, 1): 1, (1, 3): 2}
            max_split(0, 0)
            for half in range(2):
                step(0, half)
            with pool.Fori(0, 3) as i:
                for k in range(2):
                    for half in range(2):
                        step(2 * i + 1 + k, half)
            for half in range(2):
                step(7, half, more=False)
            ln_scale(2, NQ - 1)
            hot_tiles(1)
            expert_tiles(1)

        @block.scalar
        def _(act):
            def ln_apply(n, q):
                act.wait_ge(ln_nb[n], q + 1 if n < 2 else 1)
                for t in range(4 * q + 2, 4 * q + 4):
                    i1 = act.activation(xn[:, t, :], x[:, t, :], ACT.Identity, bias=nb[:, t:t + 1],
                                        scale=rs[:, t:t + 1])
                i1.then_inc(ln_xa[n], 1)

            def gate_copy(f, q):
                act.wait_ge(g_T[f], q + 1)
                if q >= 2:
                    act.wait_ge(g_lg[f], q - 1)
                act.copy(gT[:, q % 2, :], bank[q % 2][:, :]).then_inc(g_Tc[f], 1)

            def route_exp(f):
                act.wait_ge(r_sh[f], 1)
                act.activation(ex[:, :, :], sh[:, :, :], ACT.Exp).then_inc(r_ex[f], 1)

            def expert_tiles(f):
                def copy_T(t, par):
                    act.wait_ge(e_T[f], t + 1)
                    need(act, e_h[f], t - 1)
                    act.copy(xsT[:, par, :], bank[par][:, 0:P]).then_inc(e_Tc[f], 1)

                def relu(t, par, k):
                    act.wait_ge(e_h[f], t + 1)
                    need(act, e_y[f], t - 1)
                    for c in range(2):
                        mm = act.activation(hT[:, par, c, :], bank[2 + 2 * par][:, c * P:(c + 1) * P], ACT.Relu,
                                            bias=ew[:, k, HID + c:HID + c + 1])
                    mm.then_inc(e_ha[f], 1)

                def step(t, k, do_T=True, do_h=True):
                    if do_T:
                        copy_T(t + 2, k % 2)
                    if do_h:
                        relu(t + 1, (k + 1) % 2, (k + 1) % WRING)
                copy_T(0, 0)
                copy_T(1, 1)
                relu(0, 0, 0)
                for k in range(RING):
                    step(k, k)
                with act.Fori(1, NS // RING) as i:
                    for k in range(RING):
                        step(RING * i + k, k)
                for t in range(NS // RING * RING, NS):
                    step(t, t % RING, do_T=t + 2 < NS, do_h=t + 1 < NS)

            for q in range(NQ):
                ln_apply(0, q)
                if q > 0:
                    gate_copy(0, q - 1)
            gate_copy(0, NQ - 1)
            route_exp(0)
            expert_tiles(0)

            act.wait_ge(attw_s, 32)

            def quad_copy(q):
                act.wait_ge(q_T, q + 1)
                need(act, q_v, q - 1)
                act.copy(xnT[:, q % 2, :], bank[q % 2][:, :]).then_inc(q_Tc, 1)

            def quad_split1(q):
                act.wait_ge(q_qk, q + 1)
                if q >= SPL:
                    act.wait_ge(q_std[q - SPL], 128)
                for t in range(2):
                    mm = act.activation(spl[:, q % SPL, 0, t, :], bank[2 + 2 * (q % 2) + t][:, :], ACT.Identity,
                                        bias=cols[:, t:t + 1])
                mm.then_inc(q_s1, 1)

            def quad_split2(q):
                act.wait_ge(q_r, q + 1)
                act.copy(spl[:, q % SPL, 1, :, :], qkr[:, q % 2, :, :]).then_inc(q_s2, 1)
            ln_apply(1, 0)
            for q in range(NQ):
                quad_copy(q)
                if q > 0:
                    quad_split2(q - 1)
                quad_split1(q)
                if q + 1 < NQ:
                    ln_apply(1, q + 1)
            quad_split2(NQ - 1)

            def exp_unit(b, half, u):
                n = 12 * b + 6 * half + u
                act.wait_ge(a_st, n + 1)
                need(act, a_pv, 4 * (2 * b + half - 1) + (1, 1, 2, 3, 3, 4)[u]
                     if not isinstance(b, int) or 2 * b + half > 0 else 0)
                act.activation(pT[:, u, :], bank[2 + u % 2][:, :], ACT.Exp, scale=SCALE
                               ).then_inc(a_e, 1)

            def max_copy(b, half):
                act.wait_ge(a_mt, 2 * b + half + 1)
                need(act, a_m[half], 16 * b)
                act.copy(mT[:, half, :], bank[6][0:24, 0:P].bitcast(BF16)).then_inc(a_mtc, 1)

            def out_copy(b, half):
                act.wait_ge(a_pv, 4 * (2 * b + half) + 4)
                need(act, a_oT, 2 * b)
                act.copy(oT[half][:, :, :], bank[4 + half][:, :].rearrange("p (g n) -> p g n", g=2)
                         ).then_inc(a_ot, 1)

            def step(b, half, more, first=False):
                for u in range(6):
                    exp_unit(b, half, u)
                    if u == 2:
                        if half == 0:
                            max_copy(b, 1)
                        elif more:
                            max_copy(b + 1, 0)
                    if u == 3 and not (first and half == 0):
                        out_copy(b if half else b - 1, 1 - half)
                    if u == 3 and half == 1 and not first:
                        act.wait_ge(a_aT, b)
                        act.copy(anT[:, :], bank[7][:, 0:T]).then_inc(a_aTc, 1)
            max_copy(0, 0)
            for half in range(2):
                step(0, half, True, first=True)
            with act.Fori(0, 3) as i:
                for k in range(2):
                    for half in range(2):
                        step(2 * i + 1 + k, half, True)
            for half in range(2):
                step(7, half, False)
            out_copy(7, 1)
            gate_copy(1, 0)
            gate_copy(1, 1)
            act.wait_ge(a_aT, B)
            act.copy(anT[:, :], bank[7][:, 0:T]).then_inc(a_aTc, 1)
            gate_copy(1, 2)
            ln_apply(2, 3)
            gate_copy(1, 3)
            route_exp(1)
            expert_tiles(1)

        @block.vector
        def _(dve):
            def ln_stats(n, q):
                if n == 0:
                    dve.wait_ge(x_in_s[q], 16)
                elif n == 1:
                    dve.wait_ge(comb[0], q + 1)
                for t in range(4 * q, 4 * q + 4):
                    i1 = dve.bn_stats(st6[:, t, :], x[:, t, :])
                i1.then_inc(ln_st[n], 1)
                dve.wait_ge(ln_st[n], q + 1)
                for t in range(4 * q, 4 * q + 4):
                    i1 = dve.bn_aggr(mv[:, t, :], st6[:, t, :])
                i1.then_inc(ln_mv[n], 1)

            def ln_apply(n, q):
                dve.wait_ge(ln_rs[n], q + 1)
                if shared(n, q):
                    dve.scalar_tensor_tensor(nb[:, 4 * q:4 * q + 4], mv[:, 4 * q:4 * q + 4, 0], -1.0,
                                             rs[:, 4 * q:4 * q + 4], ALU.mult, ALU.mult).then_inc(ln_nb[n], 1)
                for t in range(4 * q, 4 * q + (2 if shared(n, q) else 4)):
                    i1 = dve.tensor_scalar(xn[:, t, :], x[:, t, :], mv[:, t, 0:1], rs[:, t:t + 1],
                                           ALU.subtract, ALU.mult)
                i1.then_inc(ln_xn[n], 1)

            def layernorm(n):
                ln_stats(n, 0)
                for q in range(1, NQ):
                    ln_stats(n, q)
                    ln_apply(n, q - 1)
                ln_apply(n, NQ - 1)

            def route(f):
                for q in range(NQ):
                    dve.wait_ge(g_lg[f], q + 1)
                    i1 = dve.tensor_tensor(lg[:, 4 * q:4 * q + 4, :],
                                           bank[2 + q][:, 0:4 * NE].rearrange("p (t e) -> p t e", t=4),
                                           b_gate.unsqueeze(1).broadcast_to((P, 4, NE)), ALU.add)
                n = [0]

                def chain(ins):
                    n[0] += 1
                    ins.then_inc(r_ch[f], 1)
                    dve.wait_ge(r_ch[f], n[0])
                chain(i1)
                chain(dve.tensor_reduce(mx[:, :], lg[:, :, :], AX.X, ALU.max))
                mxb = mx[:, :].unsqueeze(2).broadcast_to((P, NT, NE))
                dve.tensor_tensor(sh[:, :, :], lg[:, :, :], mxb, ALU.subtract).then_inc(r_sh[f], 1)
                chain(dve.tensor_tensor(oh[:, :, :], lg[:, :, :], mxb, ALU.is_equal))
                chain(dve.tensor_tensor(pick[:, :, :], oh[:, :, :],
                                        cst[:, C_REV:C_REV + NE].unsqueeze(1).broadcast_to((P, NT, NE)), ALU.mult))
                chain(dve.tensor_reduce(best[:, :], pick[:, :, :], AX.X, ALU.max))
                dve.tensor_tensor(onehot[:, :, :], pick[:, :, :],
                                  best[:, :].unsqueeze(2).broadcast_to((P, NT, NE)), ALU.is_equal
                                  ).then_inc(r_oh[f], 1)
                dve.wait_ge(r_cnt[f], 1)
                inside = bank[6][:, 0:P].rearrange("p (t e) -> p t e", t=NT)
                total = bank[6][:, P:2 * P].rearrange("p (t e) -> p e t", t=NT)
                chain(dve.tensor_copy(tot[:, :, :], total))
                chain(dve.tensor_tensor_scan(upto[:, :, :].rearrange("p e t -> p (e t)"),
                                             keep[:, :, :].rearrange("p e t -> p (e t)"),
                                             tot[:, :, :].rearrange("p e t -> p (e t)"),
                                             0.0, ALU.mult, ALU.add))
                dve.tensor_tensor(base[:, :, :], upto[:, :, :], tot[:, :, :], ALU.subtract).then_inc(r_rank[f], 1)
                cnt = upto[:, :, NT - 1]
                chain(dve.tensor_tensor(gtj[:, :, :], cnt.unsqueeze(2).broadcast_to((P, NE, NT)),
                                        cst[:, C_J:C_J + NT].unsqueeze(1).broadcast_to((P, NE, NT)), ALU.is_gt))
                dve.wait_ge(r_rank[f], 1)
                dve.tensor_tensor(rank[:, :, :], inside, base[:, :, :].rearrange("p e t -> p t e"), ALU.add
                                  ).then_inc(r_rank[f], 1)
                chain(dve.tensor_reduce(ntl[:, :], gtj[:, :, :], AX.X, ALU.add))
                chain(dve.tensor_tensor_scan(endt[:, :], ones8[:, :], ntl[:, :], 0.0, ALU.mult, ALU.add))
                chain(dve.tensor_tensor(begt[:, :], endt[:, :], ntl[:, :], ALU.subtract))
                dve.wait_ge(r_rank[f], 2)
                chain(dve.scalar_tensor_tensor(slotm[:, :, :], begt[:, :].unsqueeze(1).broadcast_to((P, NT, NE)),
                                               float(P), rank[:, :, :], ALU.mult, ALU.add))
                chain(dve.tensor_tensor(slotm[:, :, :], slotm[:, :, :], onehot[:, :, :], ALU.mult))
                chain(dve.tensor_reduce(slotf[:, :], slotm[:, :, :], AX.X, ALU.add))
                chain(dve.tensor_copy(sloti[:, :], slotf[:, :]))
                chain(dve.tensor_scalar(tilei[:, :], sloti[:, :], 7, None, ALU.logical_shift_right))
                chain(dve.tensor_copy(tilef[:, :], tilei[:, :]))
                chain(dve.scalar_tensor_tensor(lane[:, :], tilef[:, :], -float(P), slotf[:, :], ALU.mult, ALU.add))
                dve.tensor_tensor(dlane[:, :], cst[:, C_LANE:C_LANE + 1].broadcast_to((P, NT)), lane[:, :],
                                  ALU.subtract)
                dve.scalar_tensor_tensor(dtile[:, :], tilef[:, :], -float(P), cst[:, C_TOK:C_TOK + NT],
                                         ALU.mult, ALU.add)
                dve.tensor_tensor(hot[:, :, :], tilef[:, :].unsqueeze(2).broadcast_to((P, NT, NS)),
                                        cst[:, C_T:C_T + NS].unsqueeze(1).broadcast_to((P, NT, NS)), ALU.is_equal
                                  ).then_inc(r_hot[f], 1)
                for q in range(NQ):
                    dve.tensor_tensor(hot_lane[:, 4 * q:4 * q + 4, :],
                                      lane[:, 4 * q:4 * q + 4].unsqueeze(2).broadcast_to((P, 4, P)),
                                      cst[:, C_PLACE:C_PLACE + P].unsqueeze(1).broadcast_to((P, 4, P)), ALU.is_equal
                                      ).then_inc(r_lo[f], 1)
                chain(dve.tensor_tensor(geq[:, :, :], cst[:, C_T:C_T + NS].unsqueeze(2).broadcast_to((P, NS, NE)),
                                        endt[:, :].unsqueeze(1).broadcast_to((P, NS, NE)), ALU.is_ge))
                chain(dve.tensor_reduce(tef[:, :], geq[:, :, :], AX.X, ALU.add))
                dve.tensor_scalar(te[:, :], tef[:, :], float(NE - 1), None, ALU.min).then_inc(r_te[f], 1)
                dve.wait_ge(r_inv[f], 1)
                chain(dve.tensor_tensor(tokf[:, :], bank[7][:, 0:NS], cst[:, C_SELF:C_END], ALU.add))
                chain(dve.tensor_tensor(tokf[:, :], bank[7][:, NS:2 * NS], tokf[:, :], ALU.add))
                dve.tensor_scalar(tok_g[:, :], tokf[:, :], float(NOTOK), None, ALU.min).then_inc(r_tok[f], 1)
                dve.tensor_copy(tok_s[:, :], tokf[:, :]).then_inc(r_tok[f], 1)
                dve.wait_ge(r_ex[f], 1)
                chain(dve.tensor_reduce(den[:, :], ex[:, :, :], AX.X, ALU.add))
                chain(dve.reciprocal(mx[:, :], den[:, :]))
                chain(dve.tensor_scalar(pr[:, :], mx[:, :], 0.5, None, ALU.mult))

            def expert_tiles(f):
                def relu(t, par, k):
                    dve.wait_ge(e_h[f], t + 1)
                    need(dve, e_y[f], t - 1)
                    for c in range(2, HC):
                        i1 = dve.tensor_scalar(hT[:, par, c, :], bank[3 + 2 * par][:, (c - 2) * P:(c - 1) * P],
                                               ew[:, k, HID + c:HID + c + 1], 0.0,
                                               ALU.add, ALU.max)
                    i1.then_inc(e_hd[f], 1)

                def weights(t, k):
                    e = dve.value_load(te[0:1, bass.ds(t, 1)], min_val=0, max_val=NE - 1)
                    need(dve, e_yc[f], t - WRING + 1)
                    dve.tensor_scalar(ew[:, k, :], experts[:, bass.ds(e, 1), 0:WCOLS].rearrange("p a c -> p (a c)"),
                                      1.0, None, ALU.mult).then_inc(e_w[f], 1)

                def out_copy(t, i, k):
                    dve.wait_ge(e_y[f], t + 1)
                    need(dve, e_st[f][k % OUT], 16 * (RING // OUT * i + k // OUT))
                    dve.tensor_tensor(ys_sb[:, k % OUT, :], bank[6 + k % 2][:, 0:D], ew[:, k % WRING, HID + HC:WCOLS],
                                      ALU.add).then_inc(e_yc[f], 1)

                def step(t, i, k, do_w=True, do_h=True):
                    if do_h:
                        relu(t + 1, (k + 1) % 2, (k + 1) % WRING)
                    out_copy(t, i, k)
                    if do_w:
                        weights(t + WRING, k % WRING)
                dve.wait_ge(r_te[f], 1)
                dve.wait_ge(e_all, 16 * NE)
                for t in range(WRING):
                    weights(t, t)
                relu(0, 0, 0)
                for k in range(RING):
                    step(k, 0, k)
                with dve.Fori(1, NS // RING) as i:
                    for k in range(RING):
                        step(RING * i + k, i, k)
                for t in range(NS // RING * RING, NS):
                    step(t, NS // RING, t % RING, do_w=t + WRING < NS, do_h=t + 1 < NS)

            def combine(f, q):
                dve.wait_ge(y_ld[f][q], 16)
                for t in range(4 * q, 4 * q + 4):
                    i1 = dve.scalar_tensor_tensor(x[:, t, :], yg[:, t, :], pr[:, t:t + 1], x[:, t, :],
                                                  ALU.mult, ALU.add)
                i1.then_inc(comb[f], 1)

            dve.wait_ge(cst_s, 16)
            dve.tensor_copy(cb[:, :], cst[:, 0:C_J]).then_inc(cb_s, 1)
            dve.memset(keep[:, :, :], 1.0).then_inc(cb_s, 1)
            dve.memset(ones8[:, :], 1.0).then_inc(cb_s, 1)
            dve.wait_ge(cb_s, 3)
            dve.memset(keep[:, :, 0:1], 0.0).then_inc(cb_s, 1)
            layernorm(0)
            dve.wait_ge(gate_s, 32)
            dve.wait_ge(attw_s, 32)
            dve.tensor_scalar(wt[:, 0:3, :], wt[:, 0:3, :], cols[:, 2:3], None, ALU.mult).then_inc(w_nw, 1)
            route(0)
            expert_tiles(0)

            def quad_rest(q):
                par = q % 2
                dve.wait_ge(q_v, q + 1)
                dve.tensor_tensor(v[:, 4 * q:4 * q + 4, :], bank[6 + par][:, :].rearrange("p (t d) -> p t d", t=4),
                                  bv.unsqueeze(1).broadcast_to((P, 4, D)), ALU.add).then_inc(q_vc, 1)
                dve.wait_ge(q_s1, q + 1)
                need(dve, q_spl, q - 1)
                for t in range(2):
                    i1 = dve.scalar_tensor_tensor(qkr[:, par, t, :], bank[2 + 2 * par + t][:, :], cols[:, t:t + 1],
                                                  spl[:, q % SPL, 0, t, :], ALU.add, ALU.subtract)
                i1.then_inc(q_r, 1)

            def quad_split3(q):
                par = q % 2
                dve.wait_ge(q_s2, q + 1)
                dve.tensor_copy(spl[:, q % SPL, 2, 1, :], spl[:, q % SPL, 0, 1, :])
                dve.tensor_copy(spl[:, q % SPL, 2, 0, :], spl[:, q % SPL, 1, 0, :])
                dve.tensor_tensor(spl[:, q % SPL, 3, :, :], qkr[:, par, :, :], spl[:, q % SPL, 1, :, :],
                                  ALU.subtract).then_inc(q_spl, 1)

            def max_unit(b, half, u):
                dve.wait_ge(a_s, 12 * b + 6 * half + u + 1)
                pp, w = divmod(u, 3)
                if u == 0:
                    need(dve, a_mb, 2 * b + half - 1)
                if w < 2:
                    dve.tensor_reduce(mh[:, half, 1, :, 2 * pp + w],
                                      bank[u % 2][:, :].rearrange("p (h n) -> p h n", h=2), AX.X, ALU.max
                                      ).then_inc(a_mx, 1)
                else:
                    dve.tensor_reduce(mh[:, half, 0, :, 2 * pp:2 * pp + 2].rearrange("p j i -> p i j"),
                                      bank[u % 2][:, :].rearrange("p (h n) -> p h n", h=4), AX.X, ALU.max
                                      ).then_inc(a_mx, 1)

            for q in range(NQ + 2):
                if q < NQ:
                    combine(0, q)
                    ln_stats(1, q)
                if q >= 3:
                    quad_split3(q - 3)
                if 1 <= q <= NQ:
                    ln_apply(1, q - 1)
                if q >= 2:
                    quad_rest(q - 2)
            max_unit(0, 0, 0)
            max_unit(0, 0, 1)
            quad_split3(NQ - 1)

            def v_spread(b, k):
                need(dve, a_pv, 8 * (b - 1))
                dve.tensor_scalar(va[:, k, :, :, 0:HD], v[:, bass.ds(2 * b, 2), :].rearrange(
                    "p t (h d) -> p t h d", h=NH), 1.0, None, ALU.mult).then_inc(a_va, 1)

            def normalise(b, qt):
                dve.wait_ge(a_oT, 2 * b + qt + 1)
                o = bank[7 - qt][:, :].rearrange("p (g j c) -> p g j c", g=NPAIR, j=2)
                dve.reciprocal(rl[:, qt, :, :], o[:, :, :, HD]).then_inc(a_rl, 1)
                dve.wait_ge(a_rl, 2 * b + qt + 1)
                dve.tensor_tensor(an[:, qt, :].rearrange("p (j g d) -> p g j d", j=2, g=NPAIR), o[:, :, :, 0:HD],
                                  rl[:, qt, :, :].unsqueeze(3).broadcast_to((P, NPAIR, 2, HD)), ALU.mult
                                  ).then_inc(a_an, 1)

            def add_out(b):
                dve.wait_ge(a_wo, b + 1)
                dve.tensor_tensor(x[:, bass.ds(2 * b, 2), :],
                                  bank[7][:, 0:2 * D].rearrange("p (t d) -> p t d", t=2),
                                  x[:, bass.ds(2 * b, 2), :], ALU.add).then_inc(a_x, 1)

            def step(b, k, half, more, first=False):
                for u in range(6):
                    if more:
                        max_unit(b + 1, half, u)
                    if more and half == 0 and u == 2:
                        v_spread(b + 1, 1 - k)
                    if not first:
                        if half == 0 and u == 5:
                            normalise(b - 1, 0)
                        if half == 1 and u == 0:
                            normalise(b - 1, 1)
                        if half == 1 and u == 5:
                            add_out(b - 1)
            dve.wait_ge(static_s, 6)
            dve.wait_ge(q_vc, NQ)
            for u in range(2, 6):
                max_unit(0, 0, u)
            v_spread(0, 0)
            for u in range(6):
                max_unit(0, 1, u)
            for half in range(2):
                step(0, 0, half, True, first=True)
            dve.wait_ge(q_res, 3 * NQ)
            with dve.Fori(0, 3) as i:
                for k in range(2):
                    for half in range(2):
                        step(2 * i + 1 + k, 1 - k, half, True)
            dve.wait_ge(a_x, 6)
            ln_stats(2, 0)
            ln_stats(2, 1)
            normalise(6, 0)
            normalise(6, 1)
            ln_stats(2, 2)
            ln_apply(2, 0)
            add_out(6)
            ln_apply(2, 1)
            ln_apply(2, 2)
            normalise(7, 0)
            normalise(7, 1)
            add_out(7)
            dve.wait_ge(a_x, B)
            ln_stats(2, 3)
            ln_apply(2, 3)
            route(1)
            expert_tiles(1)
            for q in range(NQ):
                combine(1, q)

        @block.tensor
        def _(pe):
            pe.wait_ge(cst_s, 16)

            def gate_turn(f, q):
                pe.wait_ge(ln_xn[2 * f], q + 1)
                if shared(2 * f, q):
                    pe.wait_ge(ln_xa[2 * f], q + 1 if f == 0 else 1)
                if q >= 2:
                    pe.wait_ge(g_Tc[f], q - 1)
                for t in range(4):
                    mm = pe.transpose(bank[q % 2][:, t * P:(t + 1) * P], xn[:, 4 * q + t, :], ident)
                mm.then_inc(g_T[f], 1)

            def logits(f, q):
                pe.wait_ge(g_Tc[f], q + 1)
                for t in range(4):
                    mm = pe.matmul(bank[2 + q][:, t * NE:(t + 1) * NE], gT[:, q % 2, t * P:(t + 1) * P], wg[:, :],
                                   start=True, stop=True)
                mm.then_inc(g_lg[f], 1)

            def count_and_invert(f):
                pe.wait_ge(r_oh[f], 1)
                oh_ = onehot[:, :, :].rearrange("p t e -> p (t e)")
                pe.matmul(bank[6][:, 0:P], cb[:, C_UP:C_UP + P], oh_, start=True, stop=True)
                pe.matmul(bank[6][:, P:2 * P], cb[:, C_ONE:C_ONE + P], oh_, start=True, stop=True
                          ).then_inc(r_cnt[f], 1)
                pe.wait_ge(r_hi[f], 1)
                for t in range(NT):
                    if t % 4 == 0:
                        pe.wait_ge(r_lo[f], t // 4 + 1)
                    mm = pe.matmul(bank[7][:, 0:2 * NS], hot_lane[:, t, :],
                                   hot_tile[:, t, :, :].rearrange("p n s -> p (n s)"),
                                   start=(t == 0), stop=(t == NT - 1))
                mm.then_inc(r_inv[f], 1)

            def expert_tiles(f):
                def turn(t, i, k):
                    pe.wait_ge(e_xs[f][k], 16 * (i + 1))
                    need(pe, e_Tc[f], t - 1)
                    pe.transpose(bank[k % 2][:, 0:P], xs_sb[:, k, :], ident).then_inc(e_T[f], 1)

                def hidden(t, i, k):
                    pe.wait_ge(e_Tc[f], t + 1)
                    pe.wait_ge(e_w[f], t + 1)
                    need(pe, e_ha[f], t - 1)
                    need(pe, e_hd[f], t - 1)
                    for c in range(HC):
                        mm = pe.matmul(bank[2 + 2 * (k % 2) + c // 2][:, (c % 2) * P:(c % 2 + 1) * P],
                                       ew[:, k % WRING, c * P:(c + 1) * P], xsT[:, k % 2, :], start=True, stop=True)
                    mm.then_inc(e_h[f], 1)

                def output(t, k):
                    e = pe.value_load(te[0:1, bass.ds(t, 1)], min_val=0, max_val=NE - 1)
                    pe.wait_ge(e_ha[f], t + 1)
                    pe.wait_ge(e_hd[f], t + 1)
                    need(pe, e_yc[f], t - 1)
                    for c in range(HC):
                        w2 = experts[:, bass.ds(e, 1), WCOLS + c * D:WCOLS + (c + 1) * D]
                        mm = pe.matmul(bank[6 + k % 2][:, 0:D], hT[:, k % 2, c, :],
                                       w2.rearrange("p a c -> p (a c)"), start=(c == 0), stop=(c == HC - 1))
                    mm.then_inc(e_y[f], 1)

                def step(t, i, k, do_T=True, do_h=True):
                    if do_T:
                        turn(t + 2, i + (k + 2) // RING, (k + 2) % RING)
                    if do_h:
                        hidden(t + 1, i + (k + 1) // RING, (k + 1) % RING)
                    output(t, k)
                turn(0, 0, 0)
                turn(1, 0, 1)
                hidden(0, 0, 0)
                for k in range(RING):
                    step(k, 0, k)
                with pe.Fori(1, NS // RING) as i:
                    for k in range(RING):
                        step(RING * i + k, i, k)
                for t in range(NS // RING * RING, NS):
                    step(t, NS // RING, t % RING, do_T=t + 2 < NS, do_h=t + 1 < NS)

            pe.wait_ge(cb_s, 1)
            pe.wait_ge(gate_s, 32)
            gate_turn(0, 0)
            for q in range(NQ):
                if q + 1 < NQ:
                    gate_turn(0, q + 1)
                logits(0, q)
            count_and_invert(0)
            expert_tiles(0)

            pe.wait_ge(w_nw, 1)

            def quad_turn(q):
                pe.wait_ge(ln_xn[1], q + 1)
                pe.wait_ge(ln_xa[1], q + 1)
                need(pe, q_Tc, q - 1)
                for t in range(4):
                    mm = pe.transpose(bank[q % 2][:, t * P:(t + 1) * P], xn[:, 4 * q + t, :], ident)
                mm.then_inc(q_T, 1)

            def quad_qk(q):
                pe.wait_ge(q_Tc, q + 1)
                need(pe, q_r, q - 1)
                for t in range(2):
                    mm = pe.matmul(bank[2 + 2 * (q % 2) + t][:, :], wt[:, t, :], xnT[:, q % 2, :],
                                   start=True, stop=True)
                mm.then_inc(q_qk, 1)

            def quad_v(q):
                need(pe, q_vc, q - 1)
                for t in range(4):
                    mm = pe.matmul(bank[6 + q % 2][:, t * D:(t + 1) * D], xnT[:, q % 2, t * P:(t + 1) * P],
                                   wt[:, 2, :], start=True, stop=True)
                mm.then_inc(q_v, 1)
            quad_turn(0)
            for q in range(NQ):
                quad_qk(q)
                quad_v(q)
                if q + 1 < NQ:
                    quad_turn(q + 1)
            maskS = cb[:, C_MS:C_MS + P]

            def scores_q(b, bh, k, half, u):
                pp, w = divmod(u, 3)
                if u == 0:
                    pe.wait_ge(a_stk[k][half], 64 * (bh + 1))
                need(pe, a_mx, 12 * b + 6 * half + u - 1)
                o = bank[u % 2]
                if w < 2:
                    pair = 4 * half + 2 * pp + w
                    ov = o[:, :].rearrange("p (j n) -> p j n", j=2)
                    pe.matmul(ov[:, :, P:T], ident_b, maskS.unsqueeze(1).broadcast_to((P, 2, P)),
                              start=True, stop=False, **MM_BANK)
                    for j in range(2):
                        mm = pe.matmul(ov[:, j, :], qz[k][0:SROWS, half, j, pair - 4 * half, P:T],
                                       ks[k][0:SROWS, pair, :],
                                       start=False, stop=True, **MM_BANK)
                else:
                    ov = o[:, :].rearrange("p (h n) -> p h n", h=4)
                    pe.matmul(ov, ident_b, maskS.unsqueeze(1).broadcast_to((P, 4, P)),
                              start=True, stop=False, **MM_BANK)
                    for h in range(4):
                        pair = 4 * half + 2 * pp + h // 2
                        mm = pe.matmul(ov[:, h, :], qz[k][0:SROWS, half, h % 2, pair - 4 * half, 0:P],
                                       ks[k][0:SROWS, pair, 0:P],
                                       start=False, stop=True, **MM_BANK)
                mm.then_inc(a_s, 1)

            def scores_k(b, k, half, u):
                pp, w = divmod(u, 3)
                if u == 0:
                    pe.wait_ge(a_m[half], 16 * (b + 1))
                need(pe, a_e, 12 * b + 6 * half + u - 1)
                o = bank[2 + u % 2]
                if w < 2:
                    pair = 4 * half + 2 * pp + w
                    ov = o[:, :].rearrange("p (j n) -> p j n", j=2)
                    mm = pe.matmul(ov, ks[k][0:KROWS, pair, 0:P], qz[k][0:KROWS, half, :, pair - 4 * half, :],
                                   start=True, stop=True, **MM_BANK)
                else:
                    ov = o[:, :].rearrange("p (i j n) -> p i j n", i=2, j=2)
                    for i in range(2):
                        pair = 4 * half + 2 * pp + i
                        mm = pe.matmul(ov[:, i, :, :], ks[k][0:KROWS, pair, P:T],
                                       qz[k][0:KROWS, half, :, pair - 4 * half, P:T],
                                       start=True, stop=True, **MM_BANK)
                mm.then_inc(a_st, 1)

            def pv(b, k, half, pp, late):
                pe.wait_ge(a_pm, 8 * b + 4 * half + 2 * pp + 1 + late)
                if pp == 0 and not late:
                    need(pe, a_ot, 2 * b + half - 1)
                    if half == 0:
                        pe.wait_ge(a_va, b + 1)
                o = bank[4 + half]
                for h in range(4):
                    pair, j = 4 * half + 2 * pp + h // 2, h % 2
                    if late:
                        mm = pe.matmul(o[32 * h:32 * h + 32, pp * T + P:(pp + 1) * T], va[:, k, 1, 8 * j + pair, :],
                                       pT[:, 3 * pp + 2, h * P:(h + 1) * P], start=False, stop=True, **MM_BANK)
                    else:
                        mm = pe.matmul(o[32 * h:32 * h + 32, pp * T:(pp + 1) * T], va[:, k, 0, 8 * j + pair, :],
                                       pT[:, 3 * pp + h // 2, j * T:(j + 1) * T], start=True, stop=False, **MM_BANK)
                mm.then_inc(a_pv, 1)

            def turn_max(b, half):
                pe.wait_ge(a_mb, 2 * b + half + 1)
                o = bank[6][0:24, 0:P].bitcast(BF16)
                for qt in range(2):
                    mm = pe.transpose(o[:, qt * P:(qt + 1) * P],
                                      mb[:, half, qt, :, :].rearrange("p s h -> p (s h)"), ident_b)
                mm.then_inc(a_mt, 1)

            def turn_out(b, qt):
                pe.wait_ge(a_ot, 2 * b + 2)
                for g in range(4):
                    mm = pe.transpose(bank[7 - qt][:, g * P:(g + 1) * P], oT[g // 2][:, g % 2, qt * P:(qt + 1) * P],
                                      ident)
                mm.then_inc(a_oT, 1)

            def turn_norm(b):
                pe.wait_ge(a_an, 2 * b + 2)
                for qt in range(2):
                    mm = pe.transpose(bank[7][:, qt * P:(qt + 1) * P], an[:, qt, :], ident)
                mm.then_inc(a_aT, 1)

            def project(b):
                pe.wait_ge(a_aTc, b + 1)
                for qt in range(2):
                    mm = pe.matmul(bank[7][:, qt * D:(qt + 1) * D], anT[:, qt * P:(qt + 1) * P], wt[:, 3, :],
                                   start=True, stop=True)
                mm.then_inc(a_wo, 1)

            def step(b, bh, k, half, more, first=False):
                for u in range(6):
                    scores_k(b, k, half, u)
                    if more:
                        scores_q(b + 1, bh, 1 - k, half, u)
                    if u < 2 and half:
                        pv(b, k, 0, 1, u)
                    elif u < 2 and not first:
                        pv(b - 1, 1 - k, 1, 1, u)
                    if u == 2:
                        if half == 0:
                            if not first:
                                pe.wait_ge(a_mtc, 2 * b + 1)
                            turn_max(b, 1)
                        elif more:
                            if not first:
                                pe.wait_ge(a_an, 2 * b)
                            pe.wait_ge(a_mtc, 2 * b + 2)
                            turn_max(b + 1, 0)
                    if u == 3 or u == 4:
                        pv(b, k, half, 0, u - 3)
                    if half == 0 and not first:
                        if u == 4:
                            need(pe, a_x, b - 1)
                            turn_out(b - 1, 0)
                        if u == 5:
                            pe.wait_ge(a_mtc, 2 * b + 2)
                            turn_out(b - 1, 1)
                    if half == 1 and not first:
                        if u == 2:
                            turn_norm(b - 1)
                        if u == 4:
                            project(b - 1)
            for half in range(2):
                for u in range(6):
                    scores_q(0, 0, 0, half, u)
                    if half == 1 and u == 1:
                        pe.wait_ge(q_r, NQ)
                        pe.wait_ge(q_vc, NQ)
                        turn_max(0, 0)
            pe.wait_ge(a_mtc, 1)
            for half in range(2):
                step(0, 0, 0, half, True, first=True)
            with pe.Fori(0, 3) as i:
                for half in range(2):
                    step(2 * i + 1, i + 1, 1, half, True)
                for half in range(2):
                    step(2 * i + 2, i + 1, 0, half, True)
            for half in range(2):
                step(7, 3, 1, half, False)
            for late in range(2):
                pv(7, 1, 1, 1, late)
            pe.wait_ge(a_x, 7)
            turn_out(7, 0)
            turn_out(7, 1)
            pe.wait_ge(a_mx, 12 * B)
            pe.wait_ge(a_e, 12 * B)
            pe.wait_ge(a_ot, 2 * B - 1)
            gate_turn(1, 0)
            gate_turn(1, 1)
            turn_norm(7)
            logits(1, 0)
            project(7)
            logits(1, 1)
            gate_turn(1, 2)
            logits(1, 2)
            gate_turn(1, 3)
            logits(1, 3)
            count_and_invert(1)
            expert_tiles(1)


_INS = ["x", "wqkvo", "cols", "rows", "w_gate", "experts", "const"]


def kernel(L0_attn_x, L0_attn_norm_w, L0_attn_Wq, L0_attn_bq, L0_attn_Wk, L0_attn_bk, L0_attn_Wv, L0_attn_bv,
           L0_attn_Wo, L0_attn_bo, L0_ffn_w_gate, L0_ffn_b_gate, L0_ffn_W1, L0_ffn_b1, L0_ffn_W2, L0_ffn_b2):
    import concourse.bacc as bacc
    from concourse.bass_utils import run_bass_kernel_spmd

    f = lambda a: np.asarray(a)
    perm = np.arange(D).reshape(2, 2, NPAIR // 2, HD).transpose(1, 0, 3, 2).reshape(-1)
    wq, wk, wv, wo = (f(w).T for w in (L0_attn_Wq, L0_attn_Wk, L0_attn_Wv, L0_attn_Wo))
    pad = np.zeros(D - NE, f(L0_ffn_b_gate).dtype)
    w2 = f(L0_ffn_W2).reshape(NE, HC, P, D).transpose(0, 2, 1, 3).reshape(NE, P, HC * D)
    b2 = np.broadcast_to(f(L0_ffn_b2)[:, None, :], (NE, P, D))
    b1 = f(L0_ffn_b1).reshape(NE, HC, P).transpose(0, 2, 1)
    arrays = {
        "x": f(L0_attn_x).reshape(B * T, D),
        "wqkvo": np.stack([wq[:, perm], wk[:, perm], wv, wo], axis=1),
        "cols": np.stack([f(L0_attn_bq)[perm], f(L0_attn_bk)[perm], f(L0_attn_norm_w)], axis=1),
        "rows": np.concatenate([f(L0_attn_norm_w), f(L0_attn_bv), f(L0_attn_bo), f(L0_ffn_b_gate), pad]),
        "w_gate": f(L0_ffn_w_gate),
        "experts": np.concatenate([f(L0_ffn_W1), b1, b2, w2], axis=2).reshape(NE * P, ECOLS),
        "const": constants(),
    }
    nc = bacc.Bacc("TRN2", target_bir_lowering=False, num_devices=1)
    arrays = {f"in_{n}": np.ascontiguousarray(arrays[n]) for n in _INS}
    args = [nc.dram_tensor(n, a.shape, mybir.dt.from_np(a.dtype), kind="ExternalInput").ap()
            for n, a in arrays.items()]
    out = nc.dram_tensor("out_0", (B * T, D), F32, kind="ExternalOutput").ap()
    build(nc, *args, out)
    r = run_bass_kernel_spmd(nc, [arrays], core_ids=[0])
    return r.results[0]["out_0"].reshape(B, T, D)
```
